# Optimizing a Trainium2 kernel written in Bass

```python
import numpy as np
import jax
import jax.numpy as jnp

def _softmax(x, axis=-1):
    return jax.nn.softmax(x, axis=axis)

def _gelu(x):
    return jax.nn.gelu(x, approximate=True)

def _silu(x):
    return jax.nn.silu(x)

def _sigmoid(x):
    return jax.nn.sigmoid(x)

def _layernorm(x, axis=-1, eps=1e-05):
    m = jnp.mean(x, axis=axis, keepdims=True)
    v = jnp.var(x, axis=axis, keepdims=True)
    return (x - m) / jnp.sqrt(v + eps)

def _scatter_add(tgt, idx, src, axis=0):
    return tgt.at[idx].add(src)

def _segment_sum(src, seg, n):
    return jax.ops.segment_sum(src, seg, n)
kernel_name = 'mk_seq_preln_d1_jaxref_r8_37098c'

def setup_inputs(seed: int=0):
    np.random.seed(seed)
    _w = jnp.asarray

    def _L0_attn_setup():
        import jax, jax.numpy as jnp
        import numpy as np
        D_MODEL = 128
        N_HEADS = 16
        WINDOW = 32
        SEQ = 512
        BATCH = 1
        NEG_INF = -1e+30
        key = jax.random.key(seed)
        ks = jax.random.split(key, 5)
        scale = 0.02
        inp = {'x': jax.random.normal(ks[0], (BATCH, SEQ, D_MODEL), jnp.float32)}
        for i, name in enumerate(['Wq', 'Wk', 'Wv', 'Wo']):
            inp[name] = jax.random.normal(ks[1 + i], (D_MODEL, D_MODEL), jnp.float32) * scale
        for name in ['bq', 'bk', 'bv', 'bo']:
            inp[name] = jnp.zeros((D_MODEL,), jnp.float32)
        return inp
    _L0_attn_in = _L0_attn_setup()

    def _L0_ffn_setup():
        import jax, jax.numpy as jnp
        import numpy as np
        LORA_DIM = 16
        LORA_TOKEN_INDEX = 1
        B, S, D, H = (4, 256, 128, 512)
        key = jax.random.key(seed)
        ks = jax.random.split(key, 6)
        x = jax.random.normal(ks[0], (B, S, D), dtype=jnp.float32)
        W1 = jax.random.normal(ks[1], (H, D), dtype=jnp.float32) * 0.02
        b1 = jnp.zeros((H,), dtype=jnp.float32)
        W2 = jax.random.normal(ks[2], (D, H), dtype=jnp.float32) * 0.02
        b2 = jnp.zeros((D,), dtype=jnp.float32)
        scale = jnp.asarray(0.001, dtype=jnp.float32)
        return {'x': x, 'W1': W1, 'b1': b1, 'W2': W2, 'b2': b2, 'scale': scale}
    _L0_ffn_in = _L0_ffn_setup()
    _d = {'L0_attn_x': _L0_attn_in['x'], 'L0_attn_Wq': _L0_attn_in['Wq'], 'L0_attn_bq': _L0_attn_in['bq'], 'L0_attn_Wk': _L0_attn_in['Wk'], 'L0_attn_bk': _L0_attn_in['bk'], 'L0_attn_Wv': _L0_attn_in['Wv'], 'L0_attn_bv': _L0_attn_in['bv'], 'L0_attn_Wo': _L0_attn_in['Wo'], 'L0_attn_bo': _L0_attn_in['bo'], 'L0_ffn_W1': _L0_ffn_in['W1'], 'L0_ffn_b1': _L0_ffn_in['b1'], 'L0_ffn_W2': _L0_ffn_in['W2'], 'L0_ffn_b2': _L0_ffn_in['b2'], 'L0_ffn_scale': _L0_ffn_in['scale']}
    _x0 = _d['L0_attn_x']
    _d['L0_attn_x'] = jax.random.normal(jax.random.fold_in(jax.random.key(seed), 1), (1, 2048, 128), dtype=_x0.dtype)
    del _x0
    return _d

def reference(L0_attn_x, L0_attn_Wq, L0_attn_bq, L0_attn_Wk, L0_attn_bk, L0_attn_Wv, L0_attn_bv, L0_attn_Wo, L0_attn_bo, L0_ffn_W1, L0_ffn_b1, L0_ffn_W2, L0_ffn_b2, L0_ffn_scale):

    def _L0_attn_ref(x, Wq, bq, Wk, bk, Wv, bv, Wo, bo):
        import jax, jax.numpy as jnp
        import numpy as np
        D_MODEL = 128
        N_HEADS = 16
        WINDOW = 32
        SEQ = 512
        BATCH = 1
        NEG_INF = -1e+30
        B, S, D = x.shape
        H = N_HEADS
        hd = D // H
        q = (x @ Wq + bq).reshape(B, S, H, hd).transpose(0, 2, 1, 3)
        k = (x @ Wk + bk).reshape(B, S, H, hd).transpose(0, 2, 1, 3)
        v = (x @ Wv + bv).reshape(B, S, H, hd).transpose(0, 2, 1, 3)
        scale = 1.0 / jnp.sqrt(jnp.asarray(hd, x.dtype))
        scores = jnp.einsum('bhqd,bhkd->bhqk', q, k) * scale
        i = jnp.arange(S)[:, None]
        j = jnp.arange(S)[None, :]
        allowed = (j <= i) & (i - j < WINDOW)
        scores = jnp.where(allowed, scores, NEG_INF)
        attn = jax.nn.softmax(scores, axis=-1)
        out = jnp.einsum('bhqk,bhkd->bhqd', attn, v)
        out = out.transpose(0, 2, 1, 3).reshape(B, S, D)
        return out @ Wo + bo

    def _L0_ffn_ref(x, W1, b1, W2, b2, scale):
        import jax, jax.numpy as jnp
        import numpy as np
        LORA_DIM = 16
        LORA_TOKEN_INDEX = 1
        B, S, D, H = (4, 256, 128, 512)
        Bx, Sx, Dx = x.shape
        Hx = W1.shape[0]
        lt = jax.lax.dynamic_slice_in_dim(x, LORA_TOKEN_INDEX, LORA_DIM, axis=1)
        even = lt[:, ::2, :]
        odd = lt[:, 1::2, :]
        m1 = (even[:, :4, :, None] * odd[:, :4, None, :]).reshape(Bx, Hx, Dx)
        m2 = (even[:, 4:, :, None] * odd[:, 4:, None, :]).reshape(Bx, Dx, Hx)
        h = jnp.einsum('bsd,hd->bsh', x, W1) + scale * jnp.einsum('bsd,bhd->bsh', x, m1) + b1
        h = jax.nn.gelu(h, approximate=False)
        out = jnp.einsum('bsh,oh->bso', h, W2) + scale * jnp.einsum('bsh,boh->bso', h, m2) + b2
        return out
    x = L0_attn_x
    x = x + _L0_attn_ref(_layernorm(x, axis=-1), L0_attn_Wq, L0_attn_bq, L0_attn_Wk, L0_attn_bk, L0_attn_Wv, L0_attn_bv, L0_attn_Wo, L0_attn_bo)
    x = x + _L0_ffn_ref(_layernorm(x, axis=-1), L0_ffn_W1, L0_ffn_b1, L0_ffn_W2, L0_ffn_b2, L0_ffn_scale)
    return x

_drawn_inputs = setup_inputs


def setup_inputs(seed=0):
    import zlib

    import numpy as np

    out = dict(_drawn_inputs(seed))
    spreads = {'L0_attn_bq': (0.0, 0.8),
     'L0_attn_bk': (0.0, 0.8),
     'L0_attn_bv': (0.0, 0.383),
     'L0_attn_bo': (0.0, 0.1),
     'L0_ffn_b1': (0.0, 0.323),
     'L0_ffn_b2': (0.0, 0.1)}
    factors = {'L0_attn_Wq': 8.0, 'L0_attn_Wk': 8.0, 'L0_attn_Wv': 6.297}
    for name, (base, spread) in spreads.items():
        noise = np.random.default_rng([zlib.crc32(name.encode()), seed]).standard_normal(out[name].shape)
        drawn = base * np.exp(spread * noise) if base else spread * noise
        out[name] = jnp.asarray(drawn.astype(out[name].dtype))
    for name, factor in factors.items():
        out[name] = (out[name] * factor).astype(out[name].dtype)
    return out
```

```python
from contextlib import ExitStack

import concourse.bass as bass
from concourse import mybir
from concourse.alu_op_type import AluOpType as ALU

ACT = mybir.ActivationFunctionType
F32 = mybir.dt.float32
BF16 = mybir.dt.bfloat16
U32 = mybir.dt.uint32
AX = mybir.AxisListType

P = 128
D = 128
HEADS, HD = 16, 8
GH = 4
NG = HEADS // GH
WIN = 32
CHUNK = 256
BLOCKS = CHUNK // WIN
TILES = CHUNK // P
UNITS = 4
UB = BLOCKS // UNITS
KW = CHUNK + WIN
VC = GH * HD + GH
NEG = -1e30
EPS = 1e-5
HID = 512
HC = HID // P
LORA_AT = 1
FT = 4
FC = FT * P


def block_kernel(nc, x, Wq, bq, Wk, bk, Wv, bv, Wo, bo, W1, b1, W2, b2, scale, out):
    S = x.shape[1]
    NT = S // P
    NCH = S // CHUNK
    SUPER = NCH // 2
    SU = 2 * UNITS
    NU = SUPER * SU
    NF = S // FC
    x_t = x.rearrange("a (t p) d -> p (a t) d", p=P)
    out_t = out.rearrange("a (t p) d -> p (a t) d", p=P)

    with ExitStack() as ctx:
        def sb(name, shape, dt=F32):
            return ctx.enter_context(nc.sbuf_tensor(name, shape, dt))

        def two(name, shape, dt=F32):
            return [sb(f"{name}{i}", shape, dt) for i in range(2)]

        def bank(name):
            return ctx.enter_context(nc.psum_tensor(name, [P, 512], F32))

        def sem(name):
            return ctx.enter_context(nc.semaphore(name))

        x_sb = sb("x_sb", [P, NT, D])
        x_bo = sb("x_bo", [P, NT, D])
        x1 = sb("x1", [P, NT, D])
        wq, wk, wv, wo = (sb(n, [P, D]) for n in ("wq", "wk", "wv", "wo"))
        w1 = sb("w1", [P, HC, D])
        w2 = sb("w2", [P, HID])
        w1T = sb("w1T", [P, HID])
        w2T = sb("w2T", [P, HC, D])
        bqc, bkc, bvc, scale_c = (sb(n, [P, 1]) for n in ("bqc", "bkc", "bvc", "scale_c"))
        b1c = sb("b1c", [P, HC])
        bo_row, b2_row = (sb(n, [P, D]) for n in ("bo_row", "b2_row"))
        ident = sb("ident", [P, P])
        ident_bf = sb("ident_bf", [P, P], BF16)
        shift = sb("shift", [P, P])
        pick = sb("pick", [P, 2 * HC])
        ones = sb("ones", [P, P])
        half = sb("half", [P, NT])
        band = sb("band", [P, 2, WIN], BF16)
        stats1 = sb("stats1", [P, NT, 6])
        mv1 = sb("mv1", [P, NT, 2])
        var1 = sb("var1", [P, NT])
        rstd1 = sb("rstd1", [P, NT])
        xn = two("xn", [P, TILES, D])
        xT = two("xT", [P, CHUNK])
        rest = sb("rest", [P, 2, CHUNK])
        q_parts = two("q_parts", [P, 3, CHUNK], BF16)
        k_parts = two("k_parts", [P, 3, KW], BF16)
        QA = two("QA", [P, NG, GH, CHUNK], BF16)
        QB = two("QB", [P, NG, GH, CHUNK], BF16)
        KA = two("KA", [P, NG, KW], BF16)
        KB = two("KB", [P, NG, KW], BF16)
        V = two("V", [P, BLOCKS + 1, NG, VC])
        rowmax = two("rowmax", [P, UB * NG])
        centred = two("centred", [P, UB * NG, 2 * WIN])
        probs = two("probs", [P, UB * NG * 2 * WIN])
        probsT = two("probsT", [P, UB, NG, 2, WIN])
        rden = sb("rden", [P, NG, GH])
        att = two("att", [P, D])
        attT = sb("attT", [P, P])
        stats2 = sb("stats2", [P, 6])
        mv2_tile = sb("mv2_tile", [P, 2])
        mv2 = sb("mv2", [P, NT, 2])
        var2 = sb("var2", [P, NT])
        rstd2 = sb("rstd2", [P, NT])
        xn2 = two("xn2", [P, FT, D])
        x2T = two("x2T", [P, FC])
        pair1 = sb("pair1", [P, HC, D])
        pair2 = sb("pair2", [P, HC, HC, D // HC])
        hidden = two("hidden", [P, HC, FC])
        y = two("y", [P, FT, D])

        bank_s = [bank("bank_s0"), bank("bank_s1")]
        bank_o = [bank("bank_o0"), bank("bank_o1")]
        bank_t, bank_qk, bank_v, bank_w = (bank(n) for n in ("bank_t", "bank_qk", "bank_v", "bank_w"))

        qa_scr, qb_scr, ka_scr, kb_scr = (
            [nc.dram_tensor(f"{n}_scr{i}", (P, parts, width), BF16).ap() for i in range(2)]
            for n, parts, width in (("qa", 4, CHUNK), ("qb", 2, CHUNK), ("ka", 4, KW), ("kb", 2, KW)))

        x_first, x_rest, w_in = sem("x_first"), sem("x_rest"), sem("w_in")
        consts, zeroed, q_zeroed, mask_set = sem("consts"), sem("zeroed"), sem("q_zeroed"), sem("mask_set")
        zeroed_v, mask_v = sem("zeroed_v"), sem("mask_v")
        wT_ps, wT_sb = sem("wT_ps"), sem("wT_sb")
        dve_ln, var1_done, rstd1_done, xn_done = (sem(n) for n in ("dve_ln", "var1_done", "rstd1_done", "xn_done"))
        xT_ps, xT_done, qk_ps, v_ps = (sem(n) for n in ("xT_ps", "xT_done", "qk_ps", "v_ps"))
        high_done, rest_done, mid_done, parts_done = (sem(n) for n in ("high_done", "rest_done", "mid_done", "parts_done"))
        scr_in = [sem("scr_in0"), sem("scr_in1")]
        stacked = [sem("stacked0"), sem("stacked1")]
        v_done, v_set, x_bo_done = sem("v_done"), sem("v_set"), sem("x_bo_done")
        s_ps, max_done, centred_done, probs_done, probsT_done, pv_ps = (
            sem(n) for n in ("s_ps", "max_done", "centred_done", "probs_done", "probsT_done", "pv_ps"))
        rden_done, att_done, attT_ps, attT_done, wo_ps, x1_done, st2_done, ag2_done, mv2_done = (
            sem(n) for n in ("rden_done", "att_done", "attT_ps", "attT_done", "wo_ps", "x1_done", "st2_done", "ag2_done", "mv2_done"))
        var2_done, rstd2_done, xn2_done, x2T_ps, x2T_done = (
            sem(n) for n in ("var2_done", "rstd2_done", "xn2_done", "x2T_ps", "x2T_done"))
        even_ps, pairs_done, update_ps, weff_done = (
            sem(n) for n in ("even_ps", "pairs_done", "update_ps", "weff_done"))
        h_ps, hidden_done, y_ps, x1b_done, y_done = (
            sem(n) for n in ("h_ps", "hidden_done", "y_ps", "x1b_done", "y_done"))
        stored = [sem("stored0"), sem("stored1")]
        N_W = 16
        SCR = 6 * 16
        STACKS = 10 * 16

        def ge(eng, s, value):
            if not isinstance(value, int) or value > 0:
                eng.wait_ge(s, value)

        def by_query(bank_):
            return bank_[:, 0:CHUNK].rearrange("p (n q) -> p q n", q=WIN)

        def turns(eng, body):
            body(0)
            with eng.Fori(1, SUPER - 1) as turn:
                body(turn)
            body(SUPER - 1)

        def is_last(turn):
            return isinstance(turn, int) and turn == SUPER - 1

        block = ctx.enter_context(nc.Block())

        @block.sync
        def _(sp):
            sp.dma_start(x_sb[:, 0:TILES], x_t[:, 0:TILES]).then_inc(x_first, 16)
            for dst, src in ((wq[:], Wq), (wk[:], Wk), (wv[:], Wv)):
                sp.dma_start(dst, src).then_inc(w_in, 16)
            for dst, src in ((bqc, bq), (bkc, bk), (bvc, bv)):
                sp.dma_start(dst[:], src.rearrange("(p a) -> p a", a=1)).then_inc(w_in, 16)
            sp.dma_start(x_sb[:, TILES:], x_t[:, TILES:]).then_inc(x_rest, 16)
            sp.dma_start(bo_row[:], bo.partition_broadcast(P)).then_inc(w_in, 16)
            sp.dma_start(wo[:], Wo).then_inc(w_in, 16)
            sp.dma_start(w1[:], W1.rearrange("(c p) d -> p c d", p=P)).then_inc(w_in, 16)
            sp.dma_start(w2[:], W2).then_inc(w_in, 16)
            for c in range(HC):
                sp.dma_start(b1c[:, c:c + 1], b1[c * P:(c + 1) * P].rearrange("(p a) -> p a", a=1)).then_inc(w_in, 16)
            sp.dma_start(b2_row[:], b2.partition_broadcast(P)).then_inc(w_in, 16)
            sp.dma_start(scale_c[:], scale.partition_broadcast(P)).then_inc(w_in, 16)

            def restack(turn, b):
                c = 2 * turn + b
                sp.wait_ge(parts_done, c + 1)
                for rep in range(2):
                    sp.dma_start(qa_scr[b][:, rep::2], q_parts[b][:, 0:2]).then_inc(scr_in[b], 16)
                    sp.dma_start(ka_scr[b][:, 2 * rep:2 * rep + 2], k_parts[b][:, 1:3]).then_inc(scr_in[b], 16)
                sp.dma_start(qb_scr[b], q_parts[b][:, 0::2]).then_inc(scr_in[b], 16)
                sp.dma_start(kb_scr[b], k_parts[b][:, 0::2]).then_inc(scr_in[b], 16)
                if isinstance(turn, int) and turn == 0:
                    sp.wait_ge(q_zeroed, 1 + b)
                ge(sp, s_ps, UNITS * (c - 1))
                sp.wait_ge(scr_in[b], SCR * turn + SCR)
                sp.dma_start(KA[b][:], ka_scr[b].rearrange("(g r) c t -> (r c) g t", g=NG)).then_inc(stacked[b], 16)
                sp.dma_start(KB[b][0:64], kb_scr[b].rearrange("(g r) c t -> (r c) g t", g=NG)).then_inc(stacked[b], 16)
                for hh in range(GH):
                    for q, scr, n in ((QA, qa_scr, 4), (QB, qb_scr, 2)):
                        rows = scr[b].rearrange("(g h r) c t -> h (r c) g t", g=NG, h=GH)[hh]
                        sp.dma_start(q[b][n * HD * hh:n * HD * (hh + 1), :, hh, :], rows).then_inc(stacked[b], 16)

            for b in range(2):
                restack(0, b)
            with sp.Fori(1, SUPER) as turn:
                for b in range(2):
                    restack(turn, b)

            for f in range(NF):
                sp.wait_ge(y_done, f + 1)
                sp.dma_start(out_t[:, f * FT:(f + 1) * FT], y[f % 2][:]).then_inc(stored[f % 2], 16)
            for b in range(2):
                sp.wait_ge(stored[b], 16 * NF // 2)

        @block.gpsimd
        def _(pool):
            nc.gpsimd.memset(ones[:], 1.0).then_inc(zeroed, 1)
            nc.gpsimd.memset(half[:], -0.5).then_inc(zeroed, 1)
            nc.gpsimd.memset(band[:], 0.0).then_inc(zeroed, 1)
            pool.wait_ge(zeroed, 3)
            nc.gpsimd.affine_select(out=ident[:], in_=ones[:], compare_op=ALU.is_equal, fill=0.0, base=0,
                                    pattern=[[-1, P]], channel_multiplier=1).then_inc(consts, 1)
            nc.gpsimd.affine_select(out=ident_bf[:], in_=ones[:], compare_op=ALU.is_equal, fill=0.0, base=0,
                                    pattern=[[-1, P]], channel_multiplier=1).then_inc(consts, 1)
            for i, r in enumerate((64, 96)):
                pool.wait_ge(consts, 2 + 2 * i)
                nc.gpsimd.affine_select(out=band[r:r + WIN, 0], in_=band[r:r + WIN, 0], compare_op=ALU.is_ge, fill=NEG,
                                        base=0, pattern=[[-1, WIN]], channel_multiplier=1).then_inc(consts, 1)
                nc.gpsimd.affine_select(out=band[r:r + WIN, 1], in_=band[r:r + WIN, 1], compare_op=ALU.is_gt, fill=NEG,
                                        base=0, pattern=[[1, WIN]], channel_multiplier=-1).then_inc(consts, 1)
            pool.wait_ge(consts, 6)
            nc.gpsimd.affine_select(out=shift[:], in_=ones[:], compare_op=ALU.is_equal, fill=0.0, base=1,
                                    pattern=[[-1, P]], channel_multiplier=1).then_inc(consts, 1)
            nc.gpsimd.affine_select(out=pick[:], in_=ones[:, 0:2 * HC], compare_op=ALU.is_equal, fill=0.0,
                                    base=-(LORA_AT + 1), pattern=[[-2, 2 * HC]],
                                    channel_multiplier=1).then_inc(consts, 1)

            def ln1_rstd(n, t0, t1):
                pool.wait_ge(var1_done, n)
                nc.gpsimd.tensor_tensor(rstd1[:, t0:t1], var1[:, t0:t1], half[:, t0:t1], ALU.pow).then_inc(rstd1_done, 1)

            def parts(turn, b):
                c = 2 * turn + b
                pool.wait_ge(mid_done, 2 * c + 2)
                nc.gpsimd.tensor_tensor(q_parts[b][:, 2], rest[:, 0], q_parts[b][:, 1], ALU.subtract)
                nc.gpsimd.tensor_tensor(k_parts[b][:, 0, WIN:], rest[:, 1], k_parts[b][:, 1, WIN:], ALU.subtract)
                if isinstance(c, int) and c == 0:
                    nc.gpsimd.memset(k_parts[0][:, :, 0:WIN], 0.0).then_inc(parts_done, 1)
                else:
                    nc.gpsimd.tensor_copy(k_parts[b][:, :, 0:WIN], k_parts[1 - b][:, :, CHUNK:KW]).then_inc(parts_done, 1)

            pool.wait_ge(consts, 8)
            ln1_rstd(1, 0, TILES)
            for b in range(2):
                nc.gpsimd.memset(V[b][:], 0.0).then_inc(zeroed, 1)
                pool.wait_ge(zeroed, 4 + b)
                for hh in range(GH):
                    ge(pool, v_set, GH * b + hh)
                    nc.gpsimd.memset(V[b][hh * WIN:(hh + 1) * WIN, :, :, GH * HD + hh:GH * HD + hh + 1],
                                     1.0).then_inc(v_set, 1)
                pool.wait_ge(v_set, GH * (b + 1))
            ln1_rstd(2, TILES, NT)
            parts(0, 0)
            parts(0, 1)
            pool.wait_ge(w_in, 16 * N_W)
            pool.wait_ge(x_rest, 16)
            nc.gpsimd.tensor_tensor(x_bo[:], x_sb[:], bo_row[:].unsqueeze(1).to_broadcast([P, NT, D]),
                                    ALU.add).then_inc(x_bo_done, 1)
            pool.wait_ge(x_bo_done, 1)
            pool.wait_ge(s_ps, UNITS)
            nc.gpsimd.tensor_copy(KB[0][64:96, :, 0:WIN],
                                  band[64:96, 1:2].to_broadcast([WIN, NG, WIN])).then_inc(mask_set, 1)
            pool.wait_ge(mask_set, 1)
            with pool.Fori(1, SUPER) as turn:
                for b in range(2):
                    parts(turn, b)
            for half_ in range(2):
                i0, i1 = half_ * NT // 2, (half_ + 1) * NT // 2
                pool.wait_ge(var2_done, half_ + 1)
                nc.gpsimd.tensor_tensor(rstd2[:, i0:i1], var2[:, i0:i1], half[:, i0:i1], ALU.pow).then_inc(rstd2_done, 1)
                nc.gpsimd.tensor_tensor(x_bo[:, i0:i1], x1[:, i0:i1],
                                        b2_row[:].unsqueeze(1).to_broadcast([P, NT // 2, D]),
                                        ALU.add).then_inc(x1b_done, 1)

        @block.tensor
        def _(pe):
            pe.wait_ge(consts, 8)
            pe.wait_ge(w_in, 16 * N_W)
            for c in range(HC):
                nc.tensor.transpose(bank_s[0][:, c * P:(c + 1) * P], w1[:, c], ident[:])
            for c in range(HC):
                mm = nc.tensor.transpose(bank_s[1][:, c * P:(c + 1) * P], w2[:, c * P:(c + 1) * P], ident[:])
            mm.then_inc(wT_ps, 1)

            def turn_x(c, b):
                pe.wait_ge(xn_done, c + 1)
                ge(pe, xT_done, c)
                for t in range(TILES):
                    mm = nc.tensor.transpose(bank_t[:, t * P:(t + 1) * P], xn[b][:, t], ident[:])
                mm.then_inc(xT_ps, 1)

            def project(c, b):
                pe.wait_ge(xT_done, c + 1)
                ge(pe, rest_done, c)
                nc.tensor.matmul(bank_qk[:, 0:CHUNK], wq[:], xT[b][:], start=True, stop=True)
                nc.tensor.matmul(bank_qk[:, CHUNK:], wk[:], xT[b][:], start=True, stop=True).then_inc(qk_ps, 1)

            def project_v(c, b):
                ge(pe, v_done, c)
                for t in range(TILES):
                    mm = nc.tensor.matmul(bank_v[:, t * D:(t + 1) * D], xT[b][:, t * P:(t + 1) * P], wv[:],
                                          start=True, stop=True)
                mm.then_inc(v_ps, 1)

            def scores(turn, s):
                k, b, u = SU * turn + s, s // UNITS, s % UNITS
                if u == 0:
                    pe.wait_ge(stacked[b], STACKS * turn + STACKS)
                    if b == 0 and not (isinstance(turn, int) and turn == 0):
                        pe.wait_ge(mask_set, 1)
                ge(pe, centred_done, k - 1)
                for i in range(UB):
                    j = UB * u + i
                    for g in range(NG):
                        dst = bank_s[s % 2][:, (i * NG + g) * 2 * WIN:(i * NG + g + 1) * 2 * WIN]
                        nc.tensor.matmul(dst, QA[b][:, g].rearrange("p h t -> p (h t)")[:, j::BLOCKS],
                                         KA[b][:, g, j * WIN:(j + 2) * WIN], start=True, stop=False)
                        mm = nc.tensor.matmul(dst, QB[b][:, g].rearrange("p h t -> p (h t)")[:, j::BLOCKS],
                                              KB[b][:, g, j * WIN:(j + 2) * WIN], start=False, stop=True)
                mm.then_inc(s_ps, 1)

            def values(turn, s):
                k, b, u = SU * turn + s, s // UNITS, s % UNITS
                if u == 0:
                    c = 2 * turn + b
                    pe.wait_ge(v_done, c + 1)
                if s % 2 == 0:
                    ge(pe, att_done, (SU // 2) * turn + s // 2 - 1)
                pe.wait_ge(probsT_done, k + 1)
                o = bank_o[(s // 2) % 2]
                for i in range(UB):
                    j = UB * u + i
                    q = j % (P // WIN)
                    for g in range(NG):
                        for w in range(2):
                            mm = nc.tensor.matmul(o[q * WIN:(q + 1) * WIN, g * VC:(g + 1) * VC],
                                                  probsT[s % 2][:, i, g, w, :], V[b][:, j + w, g, :],
                                                  start=(w == 0), stop=(w == 1))
                mm.then_inc(pv_ps, 1)

            def turn_x2(f):
                pe.wait_ge(xn2_done, f + 1)
                ge(pe, x2T_done, f)
                for t in range(FT):
                    mm = nc.tensor.transpose(bank_t[:, t * P:(t + 1) * P], xn2[f % 2][:, t], ident[:])
                mm.then_inc(x2T_ps, 1)

            def even_tokens():
                nc.tensor.matmul(bank_qk[:, 0:D], shift[:], xn2[0][:, 0], start=True, stop=True).then_inc(even_ps, 1)

            def weight_update():
                pe.wait_ge(pairs_done, 2 * HC)
                pe.wait_ge(v_done, NCH)
                nc.tensor.matmul(bank_v[:], xn2[0][:, 0], pair1[:].rearrange("p t d -> p (t d)"),
                                 start=True, stop=True)
                nc.tensor.matmul(bank_qk[:], xn2[0][:, 0], pair2[:].rearrange("p c t i -> p (c t i)"),
                                 start=True, stop=True).then_inc(update_ps, 1)

            def turn_att(tile, odd):
                pe.wait_ge(att_done, tile + 1)
                ge(pe, x1_done, tile)
                nc.tensor.transpose(bank_w[:, 0:P], att[odd][:], ident[:]).then_inc(attT_ps, 1)

            def out_proj(tile):
                pe.wait_ge(attT_done, tile + 1)
                nc.tensor.matmul(bank_w[:, P:2 * P], attT[:], wo[:], start=True, stop=True).then_inc(wo_ps, 1)

            def step(turn, s, last):
                b, u = s // UNITS, s % UNITS
                first = isinstance(turn, int) and turn == 0
                tiles = SU // 2
                if s < SU:
                    scores(turn, s)
                    c = 2 * turn + b
                    if not (last and b == 1) and u == 0:
                        project_v(c + 1, 1 - b)
                    if not last and u == 1:
                        turn_x(c + 2, b)
                    if not last and u == 2:
                        project(c + 2, b)
                if not (first and s < 2) and s < SU + 2:
                    values(turn if s >= 2 else turn - 1, (s - 2) % SU)
                if last and s == 4:
                    turn_x2(0)
                    even_tokens()
                if last and s == 6:
                    weight_update()
                if s % 2 == 0 and not (first and s < 4):
                    turn_att(tiles * turn + s // 2 - 2, (s // 2) % 2)
                if s % 2 == 1 and not (first and s < 5):
                    out_proj(tiles * turn + (s - 1) // 2 - 2)

            pe.wait_ge(x_first, 16)
            turn_x(0, 0)
            project(0, 0)
            project_v(0, 0)
            turn_x(1, 1)
            project(1, 1)

            def body(turn):
                last = is_last(turn)
                if isinstance(turn, int) and turn == 0:
                    pe.wait_ge(wT_sb, 2)
                for s in range(SU):
                    step(turn, s, last)

            turns(pe, body)
            for s in range(SU, SU + 4):
                step(SUPER - 1, s, True)

            bank_h = [bank_s[0], bank_s[1], bank_o[0], bank_o[1]]
            bank_y = [bank_qk, bank_v]
            pe.wait_ge(weff_done, 2)

            def up(f):
                pe.wait_ge(x2T_done, f + 1)
                for c in range(HC):
                    ge(pe, hidden_done, HC * (f - 1) + c + 1)
                    nc.tensor.matmul(bank_h[c][:], w1T[:, c * P:(c + 1) * P], x2T[f % 2][:],
                                     start=True, stop=True).then_inc(h_ps, 1)

            def down(f):
                pe.wait_ge(hidden_done, HC * (f + 1))
                ge(pe, y_done, f - 1)
                for t in range(FT):
                    for c in range(HC):
                        mm = nc.tensor.matmul(bank_y[f % 2][:, t * D:(t + 1) * D],
                                              hidden[f % 2][:, c, t * P:(t + 1) * P], w2T[:, c],
                                              start=(c == 0), stop=(c == HC - 1))
                mm.then_inc(y_ps, 1)

            for f in range(NF + 1):
                if f < NF:
                    up(f)
                    if f + 1 < NF:
                        turn_x2(f + 1)
                if f >= 1:
                    down(f - 1)

        @block.scalar
        def _(act):
            def ident_act(dst, src, **kw):
                return nc.scalar.activation(dst, src, ACT.Identity, **kw)

            def copy_xT(c, b):
                act.wait_ge(xT_ps, c + 1)
                ge(act, v_ps, c - 1)
                ident_act(xT[b][:], bank_t[:, 0:CHUNK]).then_inc(xT_done, 1)

            def high(turn, b):
                c = 2 * turn + b
                act.wait_ge(qk_ps, c + 1)
                if not (isinstance(turn, int) and turn == 0):
                    act.wait_ge(scr_in[b], SCR * turn)
                ge(act, parts_done, c)
                ident_act(q_parts[b][:, 0].rearrange("p (q n) -> p q n", q=WIN), by_query(bank_qk), bias=bqc[:])
                ident_act(k_parts[b][:, 2, WIN:], bank_qk[:, CHUNK:], bias=bkc[:]).then_inc(high_done, 1)

            def spread_v(turn, b, half_):
                c = 2 * turn + b
                if half_ == 0:
                    act.wait_ge(v_ps, c + 1)
                    ge(act, pv_ps, UNITS * (c - 1))
                    if isinstance(turn, int) and turn == 0:
                        act.wait_ge(v_set, GH * (b + 1))
                    if not (isinstance(turn, int) and turn == 0 and b == 0):
                        act.wait_ge(v_done, c)
                        ident_act(V[b][:, 0], V[1 - b][:, BLOCKS])
                blocks = P // WIN
                for q in range(2 * half_, 2 * half_ + 2):
                    for hh in range(GH):
                        dst = V[b][hh * WIN:(hh + 1) * WIN, 1 + q::blocks, :, hh * HD:(hh + 1) * HD]
                        src = bank_v[q * WIN:(q + 1) * WIN, 0:TILES * D].rearrange(
                            "p (t g h d) -> p t g h d", t=TILES, g=NG, h=GH)[:, :, :, hh]
                        cp = ident_act(dst, src)
                if half_ == 1:
                    cp.then_inc(v_done, 1)

            def softmax_exp(turn, s):
                k = SU * turn + s
                act.wait_ge(centred_done, k + 1)
                ge(act, probsT_done, k - 1)
                nc.scalar.activation(probs[s % 2][:], centred[s % 2][:].rearrange("p a k -> p (a k)"), ACT.Exp,
                                     scale=float(HD) ** -0.5).then_inc(probs_done, 1)

            def copy_attT(tile):
                act.wait_ge(attT_ps, tile + 1)
                ge(act, wo_ps, tile)
                ident_act(attT[:], bank_w[:, 0:P], bias=bvc[:]).then_inc(attT_done, 1)

            act.wait_ge(wT_ps, 1)
            ident_act(w1T[:], bank_s[0][:]).then_inc(wT_sb, 1)
            ident_act(w2T[:].rearrange("p c o -> p (c o)"), bank_s[1][:]).then_inc(wT_sb, 1)
            copy_xT(0, 0)
            high(0, 0)
            copy_xT(1, 1)
            high(0, 1)
            spread_v(0, 0, 0)
            spread_v(0, 0, 1)

            def step(turn, s, last):
                b, u = s // UNITS, s % UNITS
                first = isinstance(turn, int) and turn == 0
                if s < SU:
                    c = 2 * turn + b
                    softmax_exp(turn, s)
                    if not last and u == 1:
                        copy_xT(c + 2, b)
                    if not last and u == 2:
                        high(turn + 1, b)
                    if not (last and b == 1) and u in (1, 3):
                        spread_v(turn if b == 0 else turn + 1, 1 - b, u // 2)
                if s % 2 == 1 and not (first and s < 5):
                    copy_attT((SU // 2) * turn + (s - 1) // 2 - 2)

            def body(turn):
                for s in range(SU):
                    step(turn, s, is_last(turn))

            turns(act, body)
            for s in range(SU, SU + 4):
                step(SUPER - 1, s, True)

            bank_h = [bank_s[0], bank_s[1], bank_o[0], bank_o[1]]
            for f in range(NF):
                ge(act, y_ps, f - 1)
                for c in range(HC):
                    act.wait_ge(h_ps, HC * f + c + 1)
                    nc.scalar.activation(hidden[f % 2][:, c], bank_h[c][:], ACT.Gelu,
                                         bias=b1c[:, c:c + 1]).then_inc(hidden_done, 1)

        @block.vector
        def _(dve):
            for b in range(2):
                for q in (QA, QB):
                    nc.vector.memset(q[b][:].rearrange("p g h t -> p (g h t)").bitcast(U32), 0).then_inc(zeroed_v, 1)

            def ln1_var(t0, t1):
                for t in range(t0, t1):
                    nc.vector.bn_stats(stats1[:, t], x_sb[:, t]).then_inc(dve_ln, 1)
                dve.wait_ge(dve_ln, t0 + t1)
                for t in range(t0, t1):
                    nc.vector.bn_aggr(mv1[:, t], stats1[:, t]).then_inc(dve_ln, 1)
                dve.wait_ge(dve_ln, 2 * t1)
                nc.vector.tensor_scalar(var1[:, t0:t1], mv1[:, t0:t1, 1], EPS, None, ALU.add).then_inc(var1_done, 1)

            def ln1_norm(c, b):
                ge(dve, xT_ps, c - 1)
                for t in range(TILES):
                    i = TILES * c + t
                    n = nc.vector.tensor_scalar(xn[b][:, t], x_sb[:, i], mv1[:, i, 0:1],
                                                rstd1[:, bass.ds(i, 1)], ALU.subtract, ALU.mult)
                n.then_inc(xn_done, 1)

            def split_rest(c, b):
                dve.wait_ge(high_done, c + 1)
                ge(dve, parts_done, c)
                nc.vector.scalar_tensor_tensor(rest[:, 0].rearrange("p (q n) -> p q n", q=WIN), by_query(bank_qk), bqc[:],
                                               q_parts[b][:, 0].rearrange("p (q n) -> p q n", q=WIN),
                                               ALU.add, ALU.subtract)
                nc.vector.scalar_tensor_tensor(rest[:, 1], bank_qk[:, CHUNK:], bkc[:], k_parts[b][:, 2, WIN:],
                                               ALU.add, ALU.subtract).then_inc(rest_done, 1)
                dve.wait_ge(rest_done, c + 1)
                nc.vector.tensor_copy(q_parts[b][:, 1], rest[:, 0]).then_inc(mid_done, 1)
                nc.vector.tensor_copy(k_parts[b][:, 1, WIN:], rest[:, 1]).then_inc(mid_done, 1)

            def row_max(turn, s):
                k = SU * turn + s
                dve.wait_ge(s_ps, k + 1)
                nc.vector.tensor_reduce(rowmax[s % 2][:], bank_s[s % 2][:].rearrange("p (a k) -> p a k", k=2 * WIN),
                                        AX.X, ALU.max).then_inc(max_done, 1)

            def centre(turn, s):
                k = SU * turn + s
                dve.wait_ge(max_done, k + 1)
                ge(dve, probs_done, k - 1)
                nc.vector.tensor_tensor(centred[s % 2][:], bank_s[s % 2][:].rearrange("p (a k) -> p a k", k=2 * WIN),
                                        rowmax[s % 2][:].unsqueeze(2).to_broadcast([P, UB * NG, 2 * WIN]),
                                        ALU.subtract).then_inc(centred_done, 1)

            def turn_probs(turn, s):
                k = SU * turn + s
                dve.wait_ge(probs_done, k + 1)
                ge(dve, pv_ps, k - 1)
                nc.vector.transpose(probsT[s % 2][:].rearrange("p i g w q -> p (i g w q)"),
                                    probs[s % 2][:]).then_inc(probsT_done, 1)

            def normalise(tile, odd):
                o = bank_o[odd][:, 0:NG * VC].rearrange("p (g c) -> p g c", g=NG)
                dve.wait_ge(pv_ps, 2 * tile + 2)
                nc.vector.reciprocal(rden[:], o[:, :, GH * HD:]).then_inc(rden_done, 1)
                dve.wait_ge(rden_done, tile + 1)
                ge(dve, attT_ps, tile - 1)
                nc.vector.tensor_tensor(att[odd][:].rearrange("p (g h d) -> p g h d", g=NG, h=GH),
                                        o[:, :, 0:GH * HD].rearrange("p g (h d) -> p g h d", h=GH),
                                        rden[:].unsqueeze(3).to_broadcast([P, NG, GH, HD]),
                                        ALU.mult).then_inc(att_done, 1)

            def residual(tile):
                dve.wait_ge(wo_ps, tile + 1)
                nc.vector.tensor_tensor(x1[:, tile], bank_w[:, P:2 * P], x_bo[:, tile], ALU.add).then_inc(x1_done, 1)

            def var2_plus(half_):
                i0, i1 = half_ * NT // 2, (half_ + 1) * NT // 2
                dve.wait_ge(mv2_done, i1)
                nc.vector.tensor_scalar(var2[:, i0:i1], mv2[:, i0:i1, 1], EPS, None, ALU.add).then_inc(var2_done, 1)

            def ln2_norm(f):
                ge(dve, x2T_ps, f - 1)
                for t in range(FT):
                    i = FT * f + t
                    n = nc.vector.tensor_scalar(xn2[f % 2][:, t], x1[:, i], mv2[:, i, 0:1], rstd2[:, i:i + 1],
                                                ALU.subtract, ALU.mult)
                n.then_inc(xn2_done, 1)

            def copy_x2T(f):
                dve.wait_ge(x2T_ps, f + 1)
                ge(dve, h_ps, HC * (f - 1))
                nc.vector.tensor_copy(x2T[f % 2][:], bank_t[:]).then_inc(x2T_done, 1)

            def token_pairs():
                dve.wait_ge(even_ps, 1)
                for t in range(HC):
                    nc.vector.tensor_scalar(pair1[:, t], bank_qk[:, 0:D], pick[:, t:t + 1], None,
                                            ALU.mult).then_inc(pairs_done, 1)
                for t in range(HC):
                    nc.vector.tensor_scalar(pair2[:, :, t], bank_qk[:, 0:D].rearrange("p (i c) -> p c i", c=HC),
                                            pick[:, HC + t:HC + t + 1], None, ALU.mult).then_inc(pairs_done, 1)

            def update_weights():
                dve.wait_ge(update_ps, 1)
                nc.vector.scalar_tensor_tensor(w1T[:], bank_v[:], scale_c[:], w1T[:], ALU.mult,
                                               ALU.add).then_inc(weff_done, 1)
                w2T_flat = w2T[:].rearrange("p c o -> p (c o)")
                nc.vector.scalar_tensor_tensor(w2T_flat, bank_qk[:], scale_c[:], w2T_flat, ALU.mult,
                                               ALU.add).then_inc(weff_done, 1)

            dve.wait_ge(x_first, 16)
            ln1_var(0, TILES)
            dve.wait_ge(consts, 8)
            dve.wait_ge(zeroed_v, 4)
            for b in range(2):
                qb = QB[b][:].rearrange("p g h (q n e) -> p (g h) n e q", e=2, q=WIN)
                for e in range(2):
                    r = 64 + 32 * e
                    nc.vector.tensor_copy(qb[r:r + WIN, :, :, e], ident_bf[r:r + WIN, r:r + WIN].unsqueeze(1)
                                          .unsqueeze(1).to_broadcast([WIN, NG * GH, BLOCKS // 2, WIN]))
                    for g in range(NG):
                        blocks = KB[b][r:r + WIN, g].rearrange("p (n q) -> p n q", q=WIN)
                        nc.vector.tensor_copy(blocks[:, 1 - e::2], band[r:r + WIN, 0:1].to_broadcast(
                            [WIN, len(range(1 - e, BLOCKS + 1, 2)), WIN]))
                        cp = nc.vector.tensor_copy(blocks[:, e::2], band[r:r + WIN, 1:2].to_broadcast(
                            [WIN, len(range(e, BLOCKS + 1, 2)), WIN]))
                if b == 0:
                    cp.then_inc(mask_v, 1)
                    dve.wait_ge(mask_v, 1)
                    nc.vector.memset(KB[0][64:96, :, 0:WIN], NEG).then_inc(q_zeroed, 1)
                else:
                    cp.then_inc(q_zeroed, 1)
            dve.wait_ge(rstd1_done, 1)
            ln1_norm(0, 0)
            dve.wait_ge(x_rest, 16)
            ln1_var(TILES, NT)
            split_rest(0, 0)
            dve.wait_ge(rstd1_done, 2)
            ln1_norm(1, 1)
            split_rest(1, 1)
            dve.wait_ge(x_bo_done, 1)

            def step(turn, s, last):
                b, u = s // UNITS, s % UNITS
                first = isinstance(turn, int) and turn == 0
                tiles = SU // 2
                tile = tiles * turn + (s - 1) // 2 - 3
                rows = s % 2 == 1 and not (first and s < 7)
                if rows:
                    dve.wait_ge(x1_done, tile + 1)
                if s < SU:
                    row_max(turn, s)
                if rows:
                    nc.vector.bn_stats(stats2[:], x1[:, tile]).then_inc(st2_done, 1)
                    dve.wait_ge(st2_done, tile + 1)
                if not (first and s < 1) and s < SU + 1:
                    turn_probs(turn if s >= 1 else turn - 1, (s - 1) % SU)
                if rows:
                    nc.vector.bn_aggr(mv2_tile[:], stats2[:]).then_inc(ag2_done, 1)
                    dve.wait_ge(ag2_done, tile + 1)
                if s < SU:
                    centre(turn, s)
                if rows:
                    nc.vector.tensor_copy(mv2[:, tile], mv2_tile[:]).then_inc(mv2_done, 1)
                if s % 2 == 0 and not (first and s < 4) and s < SU + 4:
                    normalise(tiles * turn + s // 2 - 2, (s // 2) % 2)
                if s % 2 == 0 and not (first and s < 6):
                    residual(tiles * turn + s // 2 - 3)
                if last and s == 0:
                    var2_plus(0)
                if last and s == 2:
                    dve.wait_ge(rstd2_done, 1)
                    ln2_norm(0)
                if last and s == 4:
                    ln2_norm(1)
                if last and s == 5:
                    token_pairs()
                if last and s == 7:
                    update_weights()
                if s < SU:
                    c = 2 * turn + b
                    if not last and u == 0:
                        ln1_norm(c + 2, b)
                    if not last and u == 3:
                        split_rest(c + 2, b)

            def body(turn):
                for s in range(SU):
                    step(turn, s, is_last(turn))

            turns(dve, body)
            for s in range(SU, SU + 6):
                step(SUPER - 1, s, True)

            var2_plus(1)
            copy_x2T(0)
            dve.wait_ge(rstd2_done, 2)
            bank_y = [bank_qk, bank_v]
            dve.wait_ge(x1b_done, 2)
            for f in range(NF):
                if f + 1 < NF:
                    copy_x2T(f + 1)
                if f + 2 < NF:
                    ln2_norm(f + 2)
                dve.wait_ge(y_ps, f + 1)
                ge(dve, stored[f % 2], 16 * (f // 2))
                nc.vector.tensor_tensor(y[f % 2][:].rearrange("p t d -> p (t d)"), bank_y[f % 2][:],
                                        x_bo[:, f * FT:(f + 1) * FT].rearrange("p t d -> p (t d)"),
                                        ALU.add).then_inc(y_done, 1)


_INS = ["L0_attn_x", "L0_attn_Wq", "L0_attn_bq", "L0_attn_Wk", "L0_attn_bk", "L0_attn_Wv", "L0_attn_bv",
        "L0_attn_Wo", "L0_attn_bo", "L0_ffn_W1", "L0_ffn_b1", "L0_ffn_W2", "L0_ffn_b2", "L0_ffn_scale"]


def kernel(**inputs):
    import numpy as _np
    import concourse.bacc as _bacc
    from concourse import mybir as _mybir
    from concourse.bass_utils import run_bass_kernel_spmd as _run

    nc = _bacc.Bacc("TRN2", target_bir_lowering=False, num_devices=1)
    arrays, args = {}, []
    for name in _INS:
        a = _np.ascontiguousarray(inputs[name])
        if a.ndim == 0:
            a = a.reshape(1)
        arrays[f"in_{name}_dram"] = a
        args.append(nc.dram_tensor(f"in_{name}_dram", a.shape, _mybir.dt.from_np(a.dtype), kind="ExternalInput").ap())
    shape = inputs["L0_attn_x"].shape
    args.append(nc.dram_tensor("out_0_dram", shape, F32, kind="ExternalOutput").ap())
    block_kernel(nc, *args)
    r = _run(nc, [arrays], core_ids=[0])
    return r.results[0]["out_0_dram"]
```

```python
from contextlib import ExitStack

import concourse.bass as bass
from concourse import mybir
from concourse.alu_op_type import AluOpType as ALU

ACT = mybir.ActivationFunctionType
F32 = mybir.dt.float32
BF16 = mybir.dt.bfloat16
U32 = mybir.dt.uint32
AX = mybir.AxisListType

P = 128
D = 128
HEADS, HD = 16, 8
GH = 4
NG = HEADS // GH
WIN = 32
CHUNK = 256
BLOCKS = CHUNK // WIN
TILES = CHUNK // P
UNITS = 4
UB = BLOCKS // UNITS
KW = CHUNK + WIN
VC = GH * HD + GH
NEG = -1e30
EPS = 1e-5
HID = 512
HC = HID // P
LORA_AT = 1
FT = 4
FC = FT * P


def block_kernel(nc, x, Wq, bq, Wk, bk, Wv, bv, Wo, bo, W1, b1, W2, b2, scale, out):
    S = x.shape[1]
    NT = S // P
    NCH = S // CHUNK
    SUPER = NCH // 2
    SU = 2 * UNITS
    NU = SUPER * SU
    NF = S // FC
    x_t = x.rearrange("a (t p) d -> p (a t) d", p=P)
    out_t = out.rearrange("a (t p) d -> p (a t) d", p=P)

    with ExitStack() as ctx:
        def sb(name, shape, dt=F32):
            return ctx.enter_context(nc.sbuf_tensor(name, shape, dt))

        def two(name, shape, dt=F32):
            return [sb(f"{name}{i}", shape, dt) for i in range(2)]

        def bank(name):
            return ctx.enter_context(nc.psum_tensor(name, [P, 512], F32))

        def sem(name):
            return ctx.enter_context(nc.semaphore(name))

        x_sb = sb("x_sb", [P, NT, D])
        x_bo = sb("x_bo", [P, NT, D])
        x1 = sb("x1", [P, NT, D])
        wq, wk, wv, wo = (sb(n, [P, D]) for n in ("wq", "wk", "wv", "wo"))
        w1 = sb("w1", [P, HC, D])
        w2 = sb("w2", [P, HID])
        w1T = sb("w1T", [P, HID])
        w2T = sb("w2T", [P, HC, D])
        scale_c = sb("scale_c", [P, 1])
        bias_rows = sb("bias_rows", [3 + HC, P])
        bias_cols = sb("bias_cols", [P, 3 + HC])
        bqc, bkc, bvc = (bias_cols[:, i:i + 1] for i in range(3))
        b1c = bias_cols[:, 3:]
        bo_row, b2_row = (sb(n, [P, D]) for n in ("bo_row", "b2_row"))
        ident = sb("ident", [P, P])
        ident_bf = sb("ident_bf", [P, P], BF16)
        shift = sb("shift", [P, P])
        pick = sb("pick", [P, 2 * HC])
        ones = sb("ones", [P, P])
        half = sb("half", [P, NT])
        band = sb("band", [P, 2, WIN], BF16)
        stats1 = sb("stats1", [P, NT, 6])
        mv1 = sb("mv1", [P, NT, 2])
        var1 = sb("var1", [P, NT])
        rstd1 = sb("rstd1", [P, NT])
        xn = two("xn", [P, TILES, D])
        xT = two("xT", [P, CHUNK])
        rest = sb("rest", [P, 2, CHUNK])
        q_parts = two("q_parts", [P, 3, CHUNK], BF16)
        k_parts = two("k_parts", [P, 3, KW], BF16)
        QA = two("QA", [P, NG, GH, CHUNK], BF16)
        QB = two("QB", [P, NG, GH, CHUNK], BF16)
        KA = two("KA", [P, NG, KW], BF16)
        KB = two("KB", [P, NG, KW], BF16)
        V = two("V", [P, BLOCKS + 1, NG, VC])
        negmax = two("negmax", [P, UB * NG])
        negmax_parts = two("negmax_parts", [P, 2, UB * NG], BF16)
        probs = two("probs", [P, UB * NG * 2 * WIN])
        probsT = two("probsT", [P, UB, NG, 2, WIN])
        rden = sb("rden", [P, NG, GH])
        att = two("att", [P, D])
        attT = sb("attT", [P, P])
        stats2 = sb("stats2", [P, 6])
        mv2_tile = sb("mv2_tile", [P, 2])
        mv2 = sb("mv2", [P, NT, 2])
        var2 = sb("var2", [P, NT])
        rstd2 = sb("rstd2", [P, NT])
        xn2 = two("xn2", [P, FT, D])
        x2T = two("x2T", [P, FC])
        pair1 = sb("pair1", [P, HC, D])
        pair2 = sb("pair2", [P, HC, HC, D // HC])
        hidden = two("hidden", [P, HC, FC])
        y = two("y", [P, FT, D])

        bank_s = [bank("bank_s0"), bank("bank_s1")]
        bank_o = [bank("bank_o0"), bank("bank_o1")]
        bank_t, bank_qk, bank_v, bank_w = (bank(n) for n in ("bank_t", "bank_qk", "bank_v", "bank_w"))

        qa_scr, qb_scr, ka_scr, kb_scr = (
            [nc.dram_tensor(f"{n}_scr{i}", (P, parts, width), BF16).ap() for i in range(2)]
            for n, parts, width in (("qa", 4, CHUNK), ("qb", 2, CHUNK), ("ka", 4, KW), ("kb", 2, KW)))

        x_first, x_rest, w_in = sem("x_first"), sem("x_rest"), sem("w_in")
        x_second = sem("x_second")
        w_first, bias_ps, bias_done = sem("w_first"), sem("bias_ps"), sem("bias_done")
        consts, zeroed, q_zeroed, mask_set = sem("consts"), sem("zeroed"), sem("q_zeroed"), sem("mask_set")
        zeroed_v, mask_v = sem("zeroed_v"), sem("mask_v")
        wT_ps, wT_sb = sem("wT_ps"), sem("wT_sb")
        dve_ln, var1_done, rstd1_done, xn_done = (sem(n) for n in ("dve_ln", "var1_done", "rstd1_done", "xn_done"))
        xT_ps, xT_done, qk_ps, v_ps = (sem(n) for n in ("xT_ps", "xT_done", "qk_ps", "v_ps"))
        high_done, rest_done, mid_done, parts_done = (sem(n) for n in ("high_done", "rest_done", "mid_done", "parts_done"))
        scr_in = [sem("scr_in0"), sem("scr_in1")]
        stacked = [sem("stacked0"), sem("stacked1")]
        v_done, v_set, x_bo_done = sem("v_done"), sem("v_set"), sem("x_bo_done")
        s_ps, max_done, max_high, max_parts, centred_ps, probs_done, probsT_done, pv_ps = (
            sem(n) for n in ("s_ps", "max_done", "max_high", "max_parts", "centred_ps", "probs_done", "probsT_done",
                             "pv_ps"))
        rden_done, att_done, attT_ps, attT_done, wo_ps, x1_done, st2_done, ag2_done, mv2_done = (
            sem(n) for n in ("rden_done", "att_done", "attT_ps", "attT_done", "wo_ps", "x1_done", "st2_done", "ag2_done", "mv2_done"))
        var2_done, rstd2_done, xn2_done, x2T_ps, x2T_done = (
            sem(n) for n in ("var2_done", "rstd2_done", "xn2_done", "x2T_ps", "x2T_done"))
        even_ps, pairs_done, update_ps, weff_done = (
            sem(n) for n in ("even_ps", "pairs_done", "update_ps", "weff_done"))
        h_ps, hidden_done, y_ps, x1b_done, y_done = (
            sem(n) for n in ("h_ps", "hidden_done", "y_ps", "x1b_done", "y_done"))
        stored = [sem("stored0"), sem("stored1")]
        N_FIRST, N_W = 7, 6
        SCR = 6 * 16
        STACKS = 10 * 16

        def ge(eng, s, value):
            if not isinstance(value, int) or value > 0:
                eng.wait_ge(s, value)

        def by_query(bank_):
            return bank_[:, 0:CHUNK].rearrange("p (n q) -> p q n", q=WIN)

        def turns(eng, body):
            body(0)
            with eng.Fori(1, SUPER - 1) as turn:
                body(turn)
            body(SUPER - 1)

        def is_last(turn):
            return isinstance(turn, int) and turn == SUPER - 1

        block = ctx.enter_context(nc.Block())

        @block.sync
        def _(sp):
            sp.dma_start(x_sb[:, 0:TILES], x_t[:, 0:TILES]).then_inc(x_first, 16)
            for dst, src in ((bias_rows[0:1], bq.unsqueeze(0)), (bias_rows[1:2], bk.unsqueeze(0)),
                             (bias_rows[2:3], bv.unsqueeze(0)), (bias_rows[3:], b1.rearrange("(c p) -> c p", p=P)),
                             (wq[:], Wq), (wk[:], Wk), (wv[:], Wv)):
                sp.dma_start(dst, src).then_inc(w_first, 16)
            sp.dma_start(x_sb[:, TILES:2 * TILES], x_t[:, TILES:2 * TILES]).then_inc(x_second, 16)
            sp.dma_start(x_sb[:, 2 * TILES:], x_t[:, 2 * TILES:]).then_inc(x_rest, 16)
            for dst, src in ((w1[:], W1.rearrange("(c p) d -> p c d", p=P)), (w2[:], W2), (wo[:], Wo),
                             (bo_row[:], bo.partition_broadcast(P)), (b2_row[:], b2.partition_broadcast(P)),
                             (scale_c[:], scale.partition_broadcast(P))):
                sp.dma_start(dst, src).then_inc(w_in, 16)

            def restack(turn, b):
                c = 2 * turn + b
                sp.wait_ge(parts_done, c + 1)
                for rep in range(2):
                    sp.dma_start(qa_scr[b][:, rep::2], q_parts[b][:, 0:2]).then_inc(scr_in[b], 16)
                    sp.dma_start(ka_scr[b][:, 2 * rep:2 * rep + 2], k_parts[b][:, 1:3]).then_inc(scr_in[b], 16)
                sp.dma_start(qb_scr[b], q_parts[b][:, 0::2]).then_inc(scr_in[b], 16)
                sp.dma_start(kb_scr[b], k_parts[b][:, 0::2]).then_inc(scr_in[b], 16)
                if isinstance(turn, int) and turn == 0:
                    sp.wait_ge(q_zeroed, 1 + b)
                    if b == 1:
                        sp.wait_ge(zeroed, 6)
                ge(sp, s_ps, UNITS * (c - 1))
                sp.wait_ge(scr_in[b], SCR * turn + SCR)
                sp.dma_start(KA[b][:], ka_scr[b].rearrange("(g r) c t -> (r c) g t", g=NG)).then_inc(stacked[b], 16)
                sp.dma_start(KB[b][0:64], kb_scr[b].rearrange("(g r) c t -> (r c) g t", g=NG)).then_inc(stacked[b], 16)
                for hh in range(GH):
                    for q, scr, n in ((QA, qa_scr, 4), (QB, qb_scr, 2)):
                        rows = scr[b].rearrange("(g h r) c t -> h (r c) g t", g=NG, h=GH)[hh]
                        sp.dma_start(q[b][n * HD * hh:n * HD * (hh + 1), :, hh, :], rows).then_inc(stacked[b], 16)

            for b in range(2):
                restack(0, b)
            with sp.Fori(1, SUPER) as turn:
                for b in range(2):
                    restack(turn, b)

            for f in range(NF):
                sp.wait_ge(y_done, f + 1)
                sp.dma_start(out_t[:, f * FT:(f + 1) * FT], y[f % 2][:]).then_inc(stored[f % 2], 16)
            for b in range(2):
                sp.wait_ge(stored[b], 16 * NF // 2)

        @block.gpsimd
        def _(pool):
            def ln1_rstd(n, t0, t1):
                pool.wait_ge(var1_done, n)
                nc.gpsimd.tensor_tensor(rstd1[:, t0:t1], var1[:, t0:t1], half[:, t0:t1], ALU.pow).then_inc(rstd1_done, 1)

            def parts(turn, b):
                c = 2 * turn + b
                pool.wait_ge(mid_done, c + 1)
                nc.gpsimd.tensor_tensor(q_parts[b][:, 2], rest[:, 0], q_parts[b][:, 1], ALU.subtract)
                nc.gpsimd.tensor_tensor(k_parts[b][:, 0, WIN:], rest[:, 1], k_parts[b][:, 1, WIN:], ALU.subtract)
                if isinstance(c, int) and c == 0:
                    nc.gpsimd.memset(k_parts[0][:, :, 0:WIN], 0.0).then_inc(parts_done, 1)
                else:
                    nc.gpsimd.tensor_copy(k_parts[b][:, :, 0:WIN], k_parts[1 - b][:, :, CHUNK:KW]).then_inc(parts_done, 1)

            def add_bo(t0, t1):
                nc.gpsimd.tensor_tensor(x_bo[:, t0:t1], x_sb[:, t0:t1],
                                        bo_row[:].unsqueeze(1).to_broadcast([P, t1 - t0, D]),
                                        ALU.add).then_inc(x_bo_done, 1)

            nc.gpsimd.memset(ones[:], 1.0).then_inc(zeroed, 1)
            nc.gpsimd.memset(half[:], -0.5).then_inc(zeroed, 1)
            nc.gpsimd.memset(band[:], 0.0).then_inc(zeroed, 1)
            pool.wait_ge(zeroed, 3)
            nc.gpsimd.affine_select(out=ident[:], in_=ones[:], compare_op=ALU.is_equal, fill=0.0, base=0,
                                    pattern=[[-1, P]], channel_multiplier=1).then_inc(consts, 1)
            nc.gpsimd.affine_select(out=ident_bf[:], in_=ones[:], compare_op=ALU.is_equal, fill=0.0, base=0,
                                    pattern=[[-1, P]], channel_multiplier=1).then_inc(consts, 1)
            ln1_rstd(1, 0, TILES)
            for i, r in enumerate((64, 96)):
                pool.wait_ge(consts, 2 + 2 * i)
                ge(pool, rstd1_done, 1)
                nc.gpsimd.affine_select(out=band[r:r + WIN, 0], in_=band[r:r + WIN, 0], compare_op=ALU.is_ge, fill=NEG,
                                        base=0, pattern=[[-1, WIN]], channel_multiplier=1).then_inc(consts, 1)
                nc.gpsimd.affine_select(out=band[r:r + WIN, 1], in_=band[r:r + WIN, 1], compare_op=ALU.is_gt, fill=NEG,
                                        base=0, pattern=[[1, WIN]], channel_multiplier=-1).then_inc(consts, 1)
            pool.wait_ge(consts, 6)
            ln1_rstd(2, TILES, 2 * TILES)
            nc.gpsimd.affine_select(out=shift[:], in_=ones[:], compare_op=ALU.is_equal, fill=0.0, base=1,
                                    pattern=[[-1, P]], channel_multiplier=1).then_inc(consts, 1)
            nc.gpsimd.affine_select(out=pick[:], in_=ones[:, 0:2 * HC], compare_op=ALU.is_equal, fill=0.0,
                                    base=-(LORA_AT + 1), pattern=[[-2, 2 * HC]],
                                    channel_multiplier=1).then_inc(consts, 1)
            pool.wait_ge(consts, 8)
            for b in range(2):
                nc.gpsimd.memset(V[b][:], 0.0).then_inc(zeroed, 1)
                pool.wait_ge(zeroed, 4 + b)
                for hh in range(GH):
                    ge(pool, v_set, GH * b + hh)
                    nc.gpsimd.memset(V[b][hh * WIN:(hh + 1) * WIN, :, :, GH * HD + hh:GH * HD + hh + 1],
                                     1.0).then_inc(v_set, 1)
                pool.wait_ge(v_set, GH * (b + 1))
            pool.wait_ge(w_in, 16 * N_W)
            pool.wait_ge(x_rest, 16)
            add_bo(0, 2 * TILES)
            parts(0, 0)
            nc.gpsimd.memset(QA[1][:].rearrange("p g h t -> p (g h t)").bitcast(U32), 0).then_inc(zeroed, 1)
            parts(0, 1)
            ln1_rstd(3, 2 * TILES, 4 * TILES)
            ln1_rstd(4, 4 * TILES, NT)
            pool.wait_ge(rstd1_done, 4)
            pool.wait_ge(s_ps, UNITS)
            nc.gpsimd.tensor_copy(KB[0][64:96, :, 0:WIN],
                                  band[64:96, 1:2].to_broadcast([WIN, NG, WIN])).then_inc(mask_set, 1)
            pool.wait_ge(mask_set, 1)
            add_bo(2 * TILES, 4 * TILES)
            for b in range(2):
                parts(1, b)
            add_bo(4 * TILES, NT)
            with pool.Fori(2, SUPER) as turn:
                for b in range(2):
                    parts(turn, b)
            for half_ in range(2):
                i0, i1 = half_ * NT // 2, (half_ + 1) * NT // 2
                pool.wait_ge(var2_done, half_ + 1)
                nc.gpsimd.tensor_tensor(rstd2[:, i0:i1], var2[:, i0:i1], half[:, i0:i1], ALU.pow).then_inc(rstd2_done, 1)
                nc.gpsimd.tensor_tensor(x_bo[:, i0:i1], x1[:, i0:i1],
                                        b2_row[:].unsqueeze(1).to_broadcast([P, NT // 2, D]),
                                        ALU.add).then_inc(x1b_done, 1)

        @block.tensor
        def _(pe):
            def turn_weights():
                pe.wait_ge(w_in, 16 * N_W)
                for c in range(HC):
                    nc.tensor.transpose(bank_s[0][:, c * P:(c + 1) * P], w1[:, c], ident[:])
                for c in range(HC):
                    mm = nc.tensor.transpose(bank_s[1][:, c * P:(c + 1) * P], w2[:, c * P:(c + 1) * P], ident[:])
                mm.then_inc(wT_ps, 1)

            def turn_x(c, b):
                pe.wait_ge(xn_done, c + 1)
                ge(pe, xT_done, c)
                for t in range(TILES):
                    mm = nc.tensor.transpose(bank_t[:, t * P:(t + 1) * P], xn[b][:, t], ident[:])
                mm.then_inc(xT_ps, 1)

            def project(c, b):
                pe.wait_ge(xT_done, c + 1)
                ge(pe, rest_done, c)
                nc.tensor.matmul(bank_qk[:, 0:CHUNK], wq[:], xT[b][:], start=True, stop=True)
                nc.tensor.matmul(bank_qk[:, CHUNK:], wk[:], xT[b][:], start=True, stop=True).then_inc(qk_ps, 1)

            def project_v(c, b):
                ge(pe, v_done, c)
                for t in range(TILES):
                    mm = nc.tensor.matmul(bank_v[:, t * D:(t + 1) * D], xT[b][:, t * P:(t + 1) * P], wv[:],
                                          start=True, stop=True)
                mm.then_inc(v_ps, 1)

            def scores(turn, s):
                k, b, u = SU * turn + s, s // UNITS, s % UNITS
                if u == 0:
                    pe.wait_ge(stacked[b], STACKS * turn + STACKS)
                    if b == 0 and not (isinstance(turn, int) and turn == 0):
                        pe.wait_ge(mask_set, 1)
                ge(pe, probs_done, k - 1)
                for i in range(UB):
                    j = UB * u + i
                    for g in range(NG):
                        dst = bank_s[s % 2][:, (i * NG + g) * 2 * WIN:(i * NG + g + 1) * 2 * WIN]
                        nc.tensor.matmul(dst, QA[b][:, g].rearrange("p h t -> p (h t)")[:, j::BLOCKS],
                                         KA[b][:, g, j * WIN:(j + 2) * WIN], start=(i == 0 and g == 0), stop=False,
                                         skip_group_check=True)
                        mm = nc.tensor.matmul(dst, QB[b][:, g].rearrange("p h t -> p (h t)")[:, j::BLOCKS],
                                              KB[b][:, g, j * WIN:(j + 2) * WIN], start=False, stop=False,
                                              skip_group_check=True)
                mm.then_inc(s_ps, 1)

            def centre(turn, s):
                k = SU * turn + s
                pe.wait_ge(max_parts, k + 1)
                for part in range(2):
                    mm = nc.tensor.matmul(bank_s[s % 2][:].rearrange("p (a k) -> p a k", k=2 * WIN), ident_bf[:],
                                          negmax_parts[s % 2][:, part].unsqueeze(2).to_broadcast([P, UB * NG, 2 * WIN]),
                                          start=False, stop=(part == 1), skip_group_check=True)
                mm.then_inc(centred_ps, 1)

            def values(turn, s):
                k, b, u = SU * turn + s, s // UNITS, s % UNITS
                if u == 0:
                    c = 2 * turn + b
                    pe.wait_ge(v_done, c + 1)
                if s % 2 == 0:
                    ge(pe, att_done, (SU // 2) * turn + s // 2 - 1)
                pe.wait_ge(probsT_done, k + 1)
                o = bank_o[(s // 2) % 2]
                for i in range(UB):
                    j = UB * u + i
                    q = j % (P // WIN)
                    for g in range(NG):
                        for w in range(2):
                            mm = nc.tensor.matmul(o[q * WIN:(q + 1) * WIN, g * VC:(g + 1) * VC],
                                                  probsT[s % 2][:, i, g, w, :], V[b][:, j + w, g, :],
                                                  start=(w == 0), stop=(w == 1))
                mm.then_inc(pv_ps, 1)

            def turn_x2(f):
                pe.wait_ge(xn2_done, f + 1)
                ge(pe, x2T_done, f)
                for t in range(FT):
                    mm = nc.tensor.transpose(bank_t[:, t * P:(t + 1) * P], xn2[f % 2][:, t], ident[:])
                mm.then_inc(x2T_ps, 1)

            bank_h = [bank_s[0], bank_s[1], bank_o[0], bank_o[1]]
            bank_y = [bank_qk, bank_v]

            def up(f, c):
                pe.wait_ge(x2T_done, f + 1)
                ge(pe, hidden_done, HC * (f - 1) + c + 1)
                nc.tensor.matmul(bank_h[c][:], w1T[:, c * P:(c + 1) * P], x2T[f % 2][:],
                                 start=True, stop=True).then_inc(h_ps, 1)

            def even_tokens():
                nc.tensor.matmul(bank_qk[:, 0:D], shift[:], xn2[0][:, 0], start=True, stop=True).then_inc(even_ps, 1)

            def weight_update():
                pe.wait_ge(pairs_done, 2 * HC)
                pe.wait_ge(v_done, NCH)
                nc.tensor.matmul(bank_v[:], xn2[0][:, 0], pair1[:].rearrange("p t d -> p (t d)"),
                                 start=True, stop=True)
                nc.tensor.matmul(bank_qk[:], xn2[0][:, 0], pair2[:].rearrange("p c t i -> p (c t i)"),
                                 start=True, stop=True).then_inc(update_ps, 1)

            def turn_att(tile, odd):
                pe.wait_ge(att_done, tile + 1)
                ge(pe, x1_done, tile)
                nc.tensor.transpose(bank_w[:, 0:P], att[odd][:], ident[:]).then_inc(attT_ps, 1)

            def out_proj(tile):
                pe.wait_ge(attT_done, tile + 1)
                nc.tensor.matmul(bank_w[:, P:2 * P], attT[:], wo[:], start=True, stop=True).then_inc(wo_ps, 1)

            def step(turn, s, last):
                b, u = s // UNITS, s % UNITS
                first = isinstance(turn, int) and turn == 0
                tiles = SU // 2
                if not (first and s < 1) and s < SU + 1:
                    centre(turn if s >= 1 else turn - 1, (s - 1) % SU)
                if not (first and s < 3) and s < SU + 3:
                    values(turn if s >= 3 else turn - 1, (s - 3) % SU)
                if s % 2 == 1 and not (first and s < 7):
                    out_proj(tiles * turn + (s - 7) // 2)
                if s % 2 == 0 and not (first and s < 6) and s < SU + 5:
                    turn_att(tiles * turn + (s - 6) // 2, (s - 6) // 2 % 2)
                if s < SU:
                    c = 2 * turn + b
                    if not (last and b == 1) and u == 0:
                        project_v(c + 1, 1 - b)
                    if not last and u == 0:
                        turn_x(c + 2, b)
                    if not last and u == 1:
                        project(c + 2, b)
                if s + 1 < SU:
                    scores(turn, s + 1)
                elif s + 1 == SU and not last:
                    scores(turn + 1, 0)
                if last and s == 4:
                    turn_x2(0)
                    even_tokens()
                if last and s == 6:
                    weight_update()
                if last and s == 7:
                    turn_x2(1)
                if last and s == 9:
                    pe.wait_ge(weff_done, 2)
                    pe.wait_ge(probs_done, NU)
                    up(0, 0)
                    up(0, 1)
                if last and s == 10:
                    pe.wait_ge(att_done, NT - 1)
                    up(0, 2)
                if last and s == 12:
                    pe.wait_ge(att_done, NT)
                    up(0, 3)

            pe.wait_ge(consts, 2)
            turn_x(0, 0)
            pe.wait_ge(w_first, 16 * N_FIRST)
            nc.tensor.transpose(bank_v[:, 0:3 + HC], bias_rows[:], ident[0:3 + HC, 0:3 + HC]).then_inc(bias_ps, 1)
            project(0, 0)
            turn_x(1, 1)
            project(1, 1)
            pe.wait_ge(bias_done, 1)
            project_v(0, 0)
            turn_weights()

            def body(turn):
                for s in range(SU):
                    step(turn, s, is_last(turn))

            pe.wait_ge(wT_sb, 2)
            scores(0, 0)
            turns(pe, body)
            for s in range(SU, SU + 6):
                step(SUPER - 1, s, True)

            def down(f):
                pe.wait_ge(hidden_done, HC * (f + 1))
                ge(pe, y_done, f - 1)
                for t in range(FT):
                    for c in range(HC):
                        mm = nc.tensor.matmul(bank_y[f % 2][:, t * D:(t + 1) * D],
                                              hidden[f % 2][:, c, t * P:(t + 1) * P], w2T[:, c],
                                              start=(c == 0), stop=(c == HC - 1))
                mm.then_inc(y_ps, 1)

            for f in range(1, NF + 1):
                if f < NF:
                    for c in range(HC):
                        up(f, c)
                if f + 1 < NF:
                    turn_x2(f + 1)
                down(f - 1)

        @block.scalar
        def _(act):
            def ident_act(dst, src, **kw):
                return nc.scalar.activation(dst, src, ACT.Identity, **kw)

            def copy_xT(c, b):
                act.wait_ge(xT_ps, c + 1)
                ge(act, v_ps, c - 1)
                ident_act(xT[b][:], bank_t[:, 0:CHUNK]).then_inc(xT_done, 1)

            def high(turn, b):
                c = 2 * turn + b
                act.wait_ge(qk_ps, c + 1)
                if not (isinstance(turn, int) and turn == 0):
                    act.wait_ge(scr_in[b], SCR * turn)
                ge(act, parts_done, c)
                ident_act(q_parts[b][:, 0].rearrange("p (q n) -> p q n", q=WIN), by_query(bank_qk), bias=bqc)
                ident_act(k_parts[b][:, 2, WIN:], bank_qk[:, CHUNK:], bias=bkc).then_inc(high_done, 1)

            def middle(c, b):
                act.wait_ge(rest_done, c + 1)
                ident_act(q_parts[b][:, 1], rest[:, 0])
                ident_act(k_parts[b][:, 1, WIN:], rest[:, 1]).then_inc(mid_done, 1)

            def spread_v(turn, b, half_):
                c = 2 * turn + b
                if half_ == 0:
                    act.wait_ge(v_ps, c + 1)
                    ge(act, pv_ps, UNITS * (c - 1))
                    if isinstance(turn, int) and turn == 0:
                        act.wait_ge(v_set, GH * (b + 1))
                    if not (isinstance(turn, int) and turn == 0 and b == 0):
                        act.wait_ge(v_done, c)
                        ident_act(V[b][:, 0], V[1 - b][:, BLOCKS])
                blocks = P // WIN
                for q in range(2 * half_, 2 * half_ + 2):
                    for hh in range(GH):
                        dst = V[b][hh * WIN:(hh + 1) * WIN, 1 + q::blocks, :, hh * HD:(hh + 1) * HD]
                        src = bank_v[q * WIN:(q + 1) * WIN, 0:TILES * D].rearrange(
                            "p (t g h d) -> p t g h d", t=TILES, g=NG, h=GH)[:, :, :, hh]
                        cp = ident_act(dst, src)
                if half_ == 1:
                    cp.then_inc(v_done, 1)

            def softmax_exp(turn, s):
                k = SU * turn + s
                act.wait_ge(centred_ps, k + 1)
                ge(act, probsT_done, k - 1)
                nc.scalar.activation(probs[s % 2][:], bank_s[s % 2][:], ACT.Exp,
                                     scale=float(HD) ** -0.5).then_inc(probs_done, 1)

            def copy_attT(tile):
                act.wait_ge(attT_ps, tile + 1)
                ge(act, wo_ps, tile)
                ident_act(attT[:], bank_w[:, 0:P], bias=bvc).then_inc(attT_done, 1)

            copy_xT(0, 0)
            act.wait_ge(bias_ps, 1)
            ident_act(bias_cols[:], bank_v[:, 0:3 + HC]).then_inc(bias_done, 1)
            act.wait_ge(bias_done, 1)
            high(0, 0)
            copy_xT(1, 1)
            middle(0, 0)
            high(0, 1)
            middle(1, 1)
            spread_v(0, 0, 0)
            spread_v(0, 0, 1)
            act.wait_ge(wT_ps, 1)
            ident_act(w1T[:], bank_s[0][:]).then_inc(wT_sb, 1)
            ident_act(w2T[:].rearrange("p c o -> p (c o)"), bank_s[1][:]).then_inc(wT_sb, 1)

            def step(turn, s, last):
                b, u = s // UNITS, s % UNITS
                first = isinstance(turn, int) and turn == 0
                if s % 2 == 0 and not (first and s < 6):
                    copy_attT((SU // 2) * turn + (s - 6) // 2)
                if s < SU:
                    c = 2 * turn + b
                    if not last and u == 1:
                        copy_xT(c + 2, b)
                    if not (first and s == 0):
                        softmax_exp(turn if s >= 1 else turn - 1, (s - 1) % SU)
                    if not last and u == 1:
                        high(turn + 1, b)
                    if not last and u == 2:
                        middle(c + 2, b)
                    if not (last and b == 1) and u >= 2:
                        spread_v(turn if b == 0 else turn + 1, 1 - b, u - 2)
                elif s == SU:
                    softmax_exp(turn, SU - 1)

            def body(turn):
                for s in range(SU):
                    step(turn, s, is_last(turn))

            turns(act, body)
            for s in range(SU, SU + 5):
                step(SUPER - 1, s, True)

            bank_h = [bank_s[0], bank_s[1], bank_o[0], bank_o[1]]
            for f in range(NF):
                ge(act, y_ps, f - 1)
                for c in range(HC):
                    act.wait_ge(h_ps, HC * f + c + 1)
                    nc.scalar.activation(hidden[f % 2][:, c], bank_h[c][:], ACT.Gelu,
                                         bias=b1c[:, c:c + 1]).then_inc(hidden_done, 1)

        @block.vector
        def _(dve):
            def clear(q):
                nc.vector.memset(q[:].rearrange("p g h t -> p (g h t)").bitcast(U32), 0).then_inc(zeroed_v, 1)

            def one_hot(b):
                qb = QB[b][:].rearrange("p g h (q n e) -> p (g h) n e q", e=2, q=WIN)
                for e in range(2):
                    r = 64 + 32 * e
                    hot = nc.vector.tensor_copy(qb[r:r + WIN, :, :, e], ident_bf[r:r + WIN, r:r + WIN].unsqueeze(1)
                                                .unsqueeze(1).to_broadcast([WIN, NG * GH, BLOCKS // 2, WIN]))
                return hot

            def masks(b):
                for e in range(2):
                    r = 64 + 32 * e
                    for g in range(NG):
                        blocks = KB[b][r:r + WIN, g].rearrange("p (n q) -> p n q", q=WIN)
                        for kind, n0 in ((0, 1 - e), (1, e)):
                            cp = nc.vector.tensor_copy(blocks[:, n0::2], band[r:r + WIN, kind:kind + 1].to_broadcast(
                                [WIN, len(range(n0, BLOCKS + 1, 2)), WIN]))
                return cp

            def ln1_var(t0, t1):
                for t in range(t0, t1):
                    nc.vector.bn_stats(stats1[:, t], x_sb[:, t]).then_inc(dve_ln, 1)
                dve.wait_ge(dve_ln, t0 + t1)
                for t in range(t0, t1):
                    nc.vector.bn_aggr(mv1[:, t], stats1[:, t]).then_inc(dve_ln, 1)
                dve.wait_ge(dve_ln, 2 * t1)
                nc.vector.tensor_scalar(var1[:, t0:t1], mv1[:, t0:t1, 1], EPS, None, ALU.add).then_inc(var1_done, 1)

            def ln1_norm(c, b):
                ge(dve, xT_ps, c - 1)
                for t in range(TILES):
                    i = TILES * c + t
                    n = nc.vector.tensor_scalar(xn[b][:, t], x_sb[:, i], mv1[:, i, 0:1],
                                                rstd1[:, bass.ds(i, 1)], ALU.subtract, ALU.mult)
                n.then_inc(xn_done, 1)

            def split_rest(c, b):
                dve.wait_ge(high_done, c + 1)
                ge(dve, parts_done, c)
                nc.vector.scalar_tensor_tensor(rest[:, 0].rearrange("p (q n) -> p q n", q=WIN), by_query(bank_qk), bqc,
                                               q_parts[b][:, 0].rearrange("p (q n) -> p q n", q=WIN),
                                               ALU.add, ALU.subtract)
                nc.vector.scalar_tensor_tensor(rest[:, 1], bank_qk[:, CHUNK:], bkc, k_parts[b][:, 2, WIN:],
                                               ALU.add, ALU.subtract).then_inc(rest_done, 1)

            def row_max(turn, s):
                k = SU * turn + s
                dve.wait_ge(s_ps, k + 1)
                ge(dve, max_parts, k - 1)
                nc.vector.tensor_reduce(negmax[s % 2][:], bank_s[s % 2][:].rearrange("p (a k) -> p a k", k=2 * WIN),
                                        AX.X, ALU.max, negate=True).then_inc(max_done, 1)

            def split_max(turn, s):
                k = SU * turn + s
                dve.wait_ge(max_done, k + 1)
                ge(dve, centred_ps, k - 1)
                nc.vector.tensor_copy(negmax_parts[s % 2][:, 0], negmax[s % 2][:]).then_inc(max_high, 1)
                dve.wait_ge(max_high, k + 1)
                nc.vector.tensor_tensor(negmax_parts[s % 2][:, 1], negmax[s % 2][:], negmax_parts[s % 2][:, 0],
                                        ALU.subtract).then_inc(max_parts, 1)

            def turn_probs(turn, s):
                k = SU * turn + s
                dve.wait_ge(probs_done, k + 1)
                ge(dve, pv_ps, k - 1)
                nc.vector.transpose(probsT[s % 2][:].rearrange("p i g w q -> p (i g w q)"),
                                    probs[s % 2][:]).then_inc(probsT_done, 1)

            def normalise(tile, odd):
                o = bank_o[odd][:, 0:NG * VC].rearrange("p (g c) -> p g c", g=NG)
                dve.wait_ge(pv_ps, 2 * tile + 2)
                nc.vector.reciprocal(rden[:], o[:, :, GH * HD:]).then_inc(rden_done, 1)
                dve.wait_ge(rden_done, tile + 1)
                ge(dve, attT_ps, tile - 1)
                nc.vector.tensor_tensor(att[odd][:].rearrange("p (g h d) -> p g h d", g=NG, h=GH),
                                        o[:, :, 0:GH * HD].rearrange("p g (h d) -> p g h d", h=GH),
                                        rden[:].unsqueeze(3).to_broadcast([P, NG, GH, HD]),
                                        ALU.mult).then_inc(att_done, 1)

            def residual(tile):
                dve.wait_ge(wo_ps, tile + 1)
                dve.wait_ge(x_bo_done, 3)
                nc.vector.tensor_tensor(x1[:, tile], bank_w[:, P:2 * P], x_bo[:, tile], ALU.add).then_inc(x1_done, 1)

            def var2_plus(half_):
                i0, i1 = half_ * NT // 2, (half_ + 1) * NT // 2
                dve.wait_ge(mv2_done, i1)
                nc.vector.tensor_scalar(var2[:, i0:i1], mv2[:, i0:i1, 1], EPS, None, ALU.add).then_inc(var2_done, 1)

            def ln2_norm(f):
                ge(dve, x2T_ps, f - 1)
                for t in range(FT):
                    i = FT * f + t
                    n = nc.vector.tensor_scalar(xn2[f % 2][:, t], x1[:, i], mv2[:, i, 0:1], rstd2[:, i:i + 1],
                                                ALU.subtract, ALU.mult)
                n.then_inc(xn2_done, 1)

            def copy_x2T(f):
                dve.wait_ge(x2T_ps, f + 1)
                ge(dve, h_ps, HC * (f - 1))
                nc.vector.tensor_copy(x2T[f % 2][:], bank_t[:]).then_inc(x2T_done, 1)

            def token_pairs():
                dve.wait_ge(even_ps, 1)
                for t in range(HC):
                    nc.vector.tensor_scalar(pair1[:, t], bank_qk[:, 0:D], pick[:, t:t + 1], None,
                                            ALU.mult).then_inc(pairs_done, 1)
                for t in range(HC):
                    nc.vector.tensor_scalar(pair2[:, :, t], bank_qk[:, 0:D].rearrange("p (i c) -> p c i", c=HC),
                                            pick[:, HC + t:HC + t + 1], None, ALU.mult).then_inc(pairs_done, 1)

            def update_weights():
                dve.wait_ge(update_ps, 1)
                nc.vector.scalar_tensor_tensor(w1T[:], bank_v[:], scale_c[:], w1T[:], ALU.mult,
                                               ALU.add).then_inc(weff_done, 1)
                w2T_flat = w2T[:].rearrange("p c o -> p (c o)")
                nc.vector.scalar_tensor_tensor(w2T_flat, bank_qk[:], scale_c[:], w2T_flat, ALU.mult,
                                               ALU.add).then_inc(weff_done, 1)

            clear(QA[0])
            dve.wait_ge(x_first, 16)
            ln1_var(0, TILES)
            clear(QB[0])
            dve.wait_ge(rstd1_done, 1)
            ln1_norm(0, 0)
            dve.wait_ge(zeroed_v, 2)
            dve.wait_ge(consts, 2)
            one_hot(0)
            dve.wait_ge(x_second, 16)
            ln1_var(TILES, 2 * TILES)
            dve.wait_ge(bias_done, 1)
            split_rest(0, 0)
            dve.wait_ge(rstd1_done, 2)
            ln1_norm(1, 1)
            dve.wait_ge(consts, 8)
            masks(0).then_inc(mask_v, 1)
            dve.wait_ge(x_rest, 16)
            ln1_var(2 * TILES, 4 * TILES)
            dve.wait_ge(mask_v, 1)
            nc.vector.memset(KB[0][64:96, :, 0:WIN], NEG).then_inc(q_zeroed, 1)
            clear(QB[1])
            split_rest(1, 1)
            dve.wait_ge(zeroed_v, 3)
            one_hot(1)
            masks(1).then_inc(q_zeroed, 1)
            ln1_var(4 * TILES, NT)
            dve.wait_ge(rstd1_done, 3)

            def step(turn, s, last):
                b, u = s // UNITS, s % UNITS
                first = isinstance(turn, int) and turn == 0
                tiles = SU // 2
                if s == 0 and not first and not last:
                    dve.wait_ge(rstd1_done, 4)
                if s < SU and not last and u == 0:
                    ln1_norm(2 * turn + b + 2, b)
                tile = tiles * turn + s // 2 - 4
                rows = s % 2 == 0 and not first
                if rows:
                    dve.wait_ge(x1_done, tile + 1)
                if s < SU:
                    row_max(turn, s)
                if rows:
                    nc.vector.bn_stats(stats2[:], x1[:, tile]).then_inc(st2_done, 1)
                if s < SU:
                    split_max(turn, s)
                if rows:
                    dve.wait_ge(st2_done, tile + 1)
                if not (first and s < 2) and s < SU + 2:
                    turn_probs(turn if s >= 2 else turn - 1, (s - 2) % SU)
                if rows:
                    nc.vector.bn_aggr(mv2_tile[:], stats2[:]).then_inc(ag2_done, 1)
                    dve.wait_ge(ag2_done, tile + 1)
                    nc.vector.tensor_scalar(mv2[:, tile], mv2_tile[:], 1.0, None, ALU.mult).then_inc(mv2_done, 1)
                if s % 2 == 1 and not (first and s < 5) and s < SU + 4:
                    normalise(tiles * turn + (s - 5) // 2, (s - 5) // 2 % 2)
                if s % 2 == 1 and not (first and s < 7):
                    residual(tiles * turn + (s - 7) // 2)
                if last and s == 0:
                    var2_plus(0)
                if last and s == 2:
                    dve.wait_ge(rstd2_done, 1)
                    ln2_norm(0)
                if last and s == 4:
                    ln2_norm(1)
                if last and s == 6:
                    copy_x2T(0)
                if last and s == 8:
                    copy_x2T(1)
                if last and s == 5:
                    token_pairs()
                if last and s == 7:
                    update_weights()
                if s < SU:
                    c = 2 * turn + b
                    if not last and u == 1:
                        split_rest(c + 2, b)

            def body(turn):
                for s in range(SU):
                    step(turn, s, is_last(turn))

            turns(dve, body)
            for s in range(SU, SU + 7):
                step(SUPER - 1, s, True)

            var2_plus(1)
            dve.wait_ge(rstd2_done, 2)
            ln2_norm(2)
            ln2_norm(3)
            copy_x2T(2)
            bank_y = [bank_qk, bank_v]
            dve.wait_ge(x1b_done, 2)
            for f in range(NF):
                dve.wait_ge(y_ps, f + 1)
                ge(dve, stored[f % 2], 16 * (f // 2))
                nc.vector.tensor_tensor(y[f % 2][:].rearrange("p t d -> p (t d)"), bank_y[f % 2][:],
                                        x_bo[:, f * FT:(f + 1) * FT].rearrange("p t d -> p (t d)"),
                                        ALU.add).then_inc(y_done, 1)
                if f == 0:
                    copy_x2T(3)


_INS = ["L0_attn_x", "L0_attn_Wq", "L0_attn_bq", "L0_attn_Wk", "L0_attn_bk", "L0_attn_Wv", "L0_attn_bv",
        "L0_attn_Wo", "L0_attn_bo", "L0_ffn_W1", "L0_ffn_b1", "L0_ffn_W2", "L0_ffn_b2", "L0_ffn_scale"]


def kernel(**inputs):
    import numpy as _np
    import concourse.bacc as _bacc
    from concourse import mybir as _mybir
    from concourse.bass_utils import run_bass_kernel_spmd as _run

    nc = _bacc.Bacc("TRN2", target_bir_lowering=False, num_devices=1)
    arrays, args = {}, []
    for name in _INS:
        a = _np.ascontiguousarray(inputs[name])
        if a.ndim == 0:
            a = a.reshape(1)
        arrays[f"in_{name}_dram"] = a
        args.append(nc.dram_tensor(f"in_{name}_dram", a.shape, _mybir.dt.from_np(a.dtype), kind="ExternalInput").ap())
    shape = inputs["L0_attn_x"].shape
    args.append(nc.dram_tensor("out_0_dram", shape, F32, kind="ExternalOutput").ap())
    block_kernel(nc, *args)
    r = _run(nc, [arrays], core_ids=[0])
    return r.results[0]["out_0_dram"]
```

```python
from contextlib import ExitStack

import concourse.bass as bass
from concourse import mybir
from concourse.alu_op_type import AluOpType as ALU

ACT = mybir.ActivationFunctionType
F32 = mybir.dt.float32
BF16 = mybir.dt.bfloat16
U32 = mybir.dt.uint32
AX = mybir.AxisListType

P = 128
D = 128
HEADS, HD = 16, 8
GH = 4
NG = HEADS // GH
WIN = 32
CHUNK = 256
BLOCKS = CHUNK // WIN
TILES = CHUNK // P
UNITS = 4
UB = BLOCKS // UNITS
KW = CHUNK + WIN
VC = GH * HD + GH
SLOTS = 8
MASK = 6
NEG = -1e30
EPS = 1e-5
HID = 512
HC = HID // P
LORA_AT = 1
FT = 4
FC = FT * P


def block_kernel(nc, x, Wq, bq, Wk, bk, Wv, bv, Wo, bo, W1, b1, W2, b2, scale, out):
    S = x.shape[1]
    NT = S // P
    NCH = S // CHUNK
    SUPER = NCH // 2
    SU = 2 * UNITS
    NU = SUPER * SU
    NF = S // FC
    x_t = x.rearrange("a (t p) d -> p (a t) d", p=P)
    out_t = out.rearrange("a (t p) d -> p (a t) d", p=P)

    with ExitStack() as ctx:
        def sb(name, shape, dt=F32):
            return ctx.enter_context(nc.sbuf_tensor(name, shape, dt))

        def two(name, shape, dt=F32):
            return [sb(f"{name}{i}", shape, dt) for i in range(2)]

        def bank(name):
            return ctx.enter_context(nc.psum_tensor(name, [P, 512], F32))

        def sem(name):
            return ctx.enter_context(nc.semaphore(name))

        x_sb = sb("x_sb", [P, NT, D])
        x_bo = sb("x_bo", [P, NT, D])
        x1 = sb("x1", [P, NT, D])
        wq, wk, wv, wo = (sb(n, [P, D]) for n in ("wq", "wk", "wv", "wo"))
        w1 = sb("w1", [P, HC, D])
        w2 = sb("w2", [P, HID])
        w1T = sb("w1T", [P, HID])
        w2T = sb("w2T", [P, HC, D])
        scale_c = sb("scale_c", [P, 1])
        bias_rows = sb("bias_rows", [3 + HC, P])
        bias_cols = sb("bias_cols", [P, 3 + HC])
        bqc, bkc, bvc = (bias_cols[:, i:i + 1] for i in range(3))
        b1c = bias_cols[:, 3:]
        bo_row, b2_row = (sb(n, [P, D]) for n in ("bo_row", "b2_row"))
        ident = sb("ident", [P, P])
        ident_bf = sb("ident_bf", [P, P], BF16)
        shift = sb("shift", [P, P])
        pick = sb("pick", [P, 2 * HC])
        ones = sb("ones", [P, P])
        half = sb("half", [P, NT])
        band = sb("band", [2 * WIN, 2, WIN], BF16)
        select = sb("select", [2 * WIN, 2, NG, WIN], BF16)
        one_hot = sb("one_hot", [P, CHUNK], BF16)
        stats1 = sb("stats1", [P, NT, 6])
        mv1 = sb("mv1", [P, NT, 2])
        var1 = sb("var1", [P, NT])
        rstd1 = sb("rstd1", [P, NT])
        xn = two("xn", [P, TILES, D])
        xT = two("xT", [P, CHUNK])
        rest = sb("rest", [P, 2, CHUNK])
        q_parts = two("q_parts", [P, SLOTS, CHUNK], BF16)
        k_parts = two("k_parts", [P, SLOTS, KW], BF16)
        QS = two("QS", [P, 2, NG, GH, CHUNK], BF16)
        KS = two("KS", [P, 2, NG, KW], BF16)
        V = two("V", [P, BLOCKS + 1, NG, VC])
        negmax = two("negmax", [P, UB * NG])
        negmax_low = two("negmax_low", [P, UB * NG], BF16)
        probs = two("probs", [P, UB * NG * 2 * WIN])
        probsT = two("probsT", [P, UB, NG, 2, WIN])
        rden = sb("rden", [P, NG, GH])
        att = two("att", [P, D])
        attT = sb("attT", [P, P])
        stats2 = sb("stats2", [P, NT, 6])
        mv2 = sb("mv2", [P, NT, 2])
        var2 = sb("var2", [P, NT])
        rstd2 = sb("rstd2", [P, NT])
        xn2 = two("xn2", [P, FT, D])
        x2T = two("x2T", [P, FC])
        pair1 = sb("pair1", [P, HC, D])
        pair2 = sb("pair2", [P, HC, HC, D // HC])
        hidden = two("hidden", [P, HC, FC])
        y = two("y", [P, FT, D])

        bank_s = [bank("bank_s0"), bank("bank_s1")]
        bank_o = [bank("bank_o0"), bank("bank_o1")]
        bank_t, bank_qk, bank_v, bank_w = (bank(n) for n in ("bank_t", "bank_qk", "bank_v", "bank_w"))

        q_scr, k_scr = (
            [nc.dram_tensor(f"{n}_scr{i}", (2 * NG, GH * HD, SLOTS // 2, width), BF16).ap() for i in range(2)]
            for n, width in (("q", CHUNK), ("k", KW)))

        x_first, x_rest, w_in = sem("x_first"), sem("x_rest"), sem("w_in")
        x_second = sem("x_second")
        w_first, bias_ps, bias_done = sem("w_first"), sem("bias_ps"), sem("bias_done")
        consts, zeroed, zeroed_pool = sem("consts"), sem("zeroed"), sem("zeroed_pool")
        one_hot_set, q_set, slots_ps, slots_set = (
            sem(n) for n in ("one_hot_set", "q_set", "slots_ps", "slots_set"))
        wT_ps, wT_sb = sem("wT_ps"), sem("wT_sb")
        dve_ln, var1_done, rstd1_done, xn_done = (sem(n) for n in ("dve_ln", "var1_done", "rstd1_done", "xn_done"))
        xT_ps, xT_done, qk_ps, v_ps = (sem(n) for n in ("xT_ps", "xT_done", "qk_ps", "v_ps"))
        x_centred, high_done, rest_done, mid_q_done, mid_done, low_q_done, low_done, repeat_done = (
            sem(n) for n in ("x_centred", "high_done", "rest_done", "mid_q_done", "mid_done", "low_q_done", "low_done",
                             "repeat_done"))
        q_in, k_in = ([sem(f"{n}_in{i}") for i in range(2)] for n in "qk")
        stacked = [sem("stacked0"), sem("stacked1")]
        v_done, v_set, x_bo_done = sem("v_done"), sem("v_set"), sem("x_bo_done")
        s_ps, max_done, max_parts, centred_ps, probs_done, probsT_done, pv_ps = (
            sem(n) for n in ("s_ps", "max_done", "max_parts", "centred_ps", "probs_done", "probsT_done",
                             "pv_ps"))
        rden_done, att_done, attT_ps, attT_done, wo_ps, x1_done, st2_done, mv2_done = (
            sem(n) for n in ("rden_done", "att_done", "attT_ps", "attT_done", "wo_ps", "x1_done", "st2_done", "mv2_done"))
        var2_done, rstd2_done, xn2_done, x2T_ps, x2T_done = (
            sem(n) for n in ("var2_done", "rstd2_done", "xn2_done", "x2T_ps", "x2T_done"))
        x2_centred = sem("x2_centred")
        even_ps, pairs_done, update_ps, weff_done = (
            sem(n) for n in ("even_ps", "pairs_done", "update_ps", "weff_done"))
        h_ps, hidden_done, y_ps, x1b_done, y_done = (
            sem(n) for n in ("h_ps", "hidden_done", "y_ps", "x1b_done", "y_done"))
        stored = [sem("stored0"), sem("stored1")]
        N_FIRST, N_W = 7, 6
        STACKS = (1 + GH) * 16

        def ge(eng, s, value):
            if not isinstance(value, int) or value > 0:
                eng.wait_ge(s, value)

        def by_query(bank_):
            return bank_[:, 0:CHUNK].rearrange("p (n q) -> p q n", q=WIN)

        def high_half(t):
            return t[:].bitcast(BF16)[:, 1::2]

        def turns(eng, body):
            body(0)
            with eng.Fori(1, SUPER - 1) as turn:
                body(turn)
            body(SUPER - 1)

        def bank_h(f, c):
            return ([bank_qk, bank_v] if f == 0 else bank_o)[c] if c < 2 else bank_s[c - 2]

        PIECES = [(f, 0, FT, (bank_qk, bank_v)[f % 2]) for f in range(NF - 1)] + [
            (NF - 1, 0, FT // 2, (bank_qk, bank_v)[(NF - 1) % 2]), (NF - 1, FT // 2, FT, bank_t)]

        def is_last(turn):
            return isinstance(turn, int) and turn == SUPER - 1

        def projects(turn, b):
            return not is_last(turn) and not (isinstance(turn, int) and turn == 0 and b == 0)

        block = ctx.enter_context(nc.Block())

        @block.sync
        def _(sp):
            sp.dma_start(x_sb[:, 0:TILES], x_t[:, 0:TILES]).then_inc(x_first, 16)
            for dst, src in ((bias_rows[0:1], bq.unsqueeze(0)), (bias_rows[1:2], bk.unsqueeze(0)),
                             (bias_rows[2:3], bv.unsqueeze(0)), (bias_rows[3:], b1.rearrange("(c p) -> c p", p=P)),
                             (wq[:], Wq), (wk[:], Wk), (wv[:], Wv)):
                sp.dma_start(dst, src).then_inc(w_first, 16)
            sp.dma_start(x_sb[:, TILES:2 * TILES], x_t[:, TILES:2 * TILES]).then_inc(x_second, 16)
            sp.dma_start(x_sb[:, 2 * TILES:], x_t[:, 2 * TILES:]).then_inc(x_rest, 16)
            for dst, src in ((w1[:], W1.rearrange("(c p) d -> p c d", p=P)), (w2[:], W2), (wo[:], Wo),
                             (bo_row[:], bo.partition_broadcast(P)), (b2_row[:], b2.partition_broadcast(P)),
                             (scale_c[:], scale.partition_broadcast(P))):
                sp.dma_start(dst, src).then_inc(w_in, 16)

            def restack(turn, b):
                c = 2 * turn + b
                if isinstance(turn, int) and turn == 0:
                    sp.wait_ge(slots_set, 2 + 2 * b)
                sp.wait_ge(repeat_done, c + 1)
                for low, scr, slots, done in ((low_q_done, q_scr[b], q_parts[b], q_in[b]),
                                              (low_done, k_scr[b], k_parts[b], k_in[b])):
                    sp.wait_ge(low, c + 1)
                    sp.dma_start(scr.rearrange("(o g) r c t -> (g r) o (c t)", o=2),
                                 slots[:].rearrange("p (o c) t -> p o (c t)", o=2)).then_inc(done, 16)
                if isinstance(turn, int) and turn == 0:
                    sp.wait_ge(q_set, 2 + b)
                    if b == 1:
                        sp.wait_ge(zeroed_pool, 1)
                ge(sp, s_ps, UNITS * (c - 1))
                sp.wait_ge(q_in[b], 16 * turn + 16)
                for hh in range(GH):
                    sp.dma_start(QS[b][hh * WIN:(hh + 1) * WIN].rearrange("p o g h t -> p (o g) h t")[:, :, hh, :],
                                 q_scr[b].rearrange("n (h r) c t -> h (r c) n t", h=GH)[hh]).then_inc(stacked[b], 16)
                sp.wait_ge(k_in[b], 16 * turn + 16)
                sp.dma_start(KS[b][:].rearrange("p o g t -> p (o g) t"),
                             k_scr[b].rearrange("n r c t -> (r c) n t")).then_inc(stacked[b], 16)

            for b in range(2):
                restack(0, b)
            with sp.Fori(1, SUPER) as turn:
                for b in range(2):
                    restack(turn, b)

            for n, (f, t0, t1, _) in enumerate(PIECES):
                sp.wait_ge(y_done, n + 1)
                sp.dma_start(out_t[:, f * FT + t0:f * FT + t1], y[f % 2][:, t0:t1]).then_inc(stored[f % 2], 16)
            for b in range(2):
                sp.wait_ge(stored[b], 16 * sum(f % 2 == b for f, *_ in PIECES))

        @block.gpsimd
        def _(pool):
            def ln1_rstd(n, t0, t1):
                pool.wait_ge(var1_done, n)
                nc.gpsimd.tensor_tensor(rstd1[:, t0:t1], var1[:, t0:t1], half[:, t0:t1], ALU.pow).then_inc(rstd1_done, 1)

            def ln1_norm(c, b):
                tiles = bass.ds(TILES * c, TILES)
                mean, rstd = (col.to_broadcast([P, TILES, D]) for col in (mv1[:, tiles, 0:1], rstd1[:, tiles].unsqueeze(2)))
                nc.gpsimd.tensor_tensor(xn[b][:], x_sb[:, tiles], mean, ALU.subtract).then_inc(x_centred, 1)
                pool.wait_ge(x_centred, c - 2)
                n = nc.gpsimd.tensor_tensor(xn[b][:], xn[b][:], rstd, ALU.mult)
                n.then_inc(xn_done, 1)

            def low_parts(turn, b):
                c = 2 * turn + b
                pool.wait_ge(mid_q_done, c + 1)
                nc.gpsimd.tensor_tensor(q_parts[b][:, 5], rest[:, 0], q_parts[b][:, 0],
                                        ALU.subtract).then_inc(low_q_done, 1)
                pool.wait_ge(mid_done, c + 1)
                nc.gpsimd.tensor_tensor(k_parts[b][:, 4, WIN:], rest[:, 1], k_parts[b][:, 0, WIN:],
                                        ALU.subtract).then_inc(low_done, 1)

            def add_bo(t0, t1):
                nc.gpsimd.tensor_tensor(x_bo[:, t0:t1], x_sb[:, t0:t1],
                                        bo_row[:].unsqueeze(1).to_broadcast([P, t1 - t0, D]),
                                        ALU.add).then_inc(x_bo_done, 1)

            nc.gpsimd.memset(ones[:], 1.0).then_inc(zeroed, 1)
            pool.wait_ge(zeroed, 1)
            nc.gpsimd.affine_select(out=ident[:], in_=ones[:], compare_op=ALU.is_equal, fill=0.0, base=0,
                                    pattern=[[-1, P]], channel_multiplier=1).then_inc(consts, 1)
            nc.gpsimd.memset(half[:], -0.5).then_inc(zeroed, 1)
            nc.gpsimd.affine_select(out=ident_bf[:], in_=ones[:], compare_op=ALU.is_equal, fill=0.0, base=0,
                                    pattern=[[-1, P]], channel_multiplier=1).then_inc(consts, 1)
            nc.gpsimd.memset(k_parts[0][:, 0:MASK, 0:WIN], 0.0).then_inc(zeroed, 1)
            nc.gpsimd.memset(k_parts[0][:, MASK:, 0:WIN], NEG).then_inc(zeroed, 1)
            pool.wait_ge(consts, 2)
            pool.wait_ge(zeroed, 4)
            nc.gpsimd.memset(band[:, 0], 0.0).then_inc(zeroed, 1)
            nc.gpsimd.memset(band[:, 1], NEG).then_inc(zeroed, 1)
            for s in range(2):
                nc.gpsimd.affine_select(out=select[:, s], in_=ones[0:2 * WIN, :].rearrange("p (g r) -> p g r", g=NG),
                                        compare_op=ALU.is_equal, fill=0.0, base=-s, pattern=[[0, NG], [-2, WIN]],
                                        channel_multiplier=1).then_inc(consts, 1)
            pool.wait_ge(zeroed, 6)
            for kind, fill in ((0, NEG), (1, 0.0)):
                nc.gpsimd.affine_select(out=band[:, kind], in_=band[:, kind], compare_op=ALU.is_ge, fill=fill,
                                        base=0, pattern=[[-1, WIN]], channel_multiplier=1).then_inc(consts, 1)
            pool.wait_ge(consts, 6)
            for kind, fill in ((0, NEG), (1, 0.0)):
                nc.gpsimd.affine_select(out=band[:, kind], in_=band[:, kind], compare_op=ALU.is_gt, fill=fill,
                                        base=WIN, pattern=[[1, WIN]], channel_multiplier=-1).then_inc(consts, 1)
            pool.wait_ge(consts, 8)
            ln1_rstd(1, 0, TILES)
            ln1_rstd(2, TILES, 2 * TILES)

            def set_v(b):
                nc.gpsimd.memset(V[b][:], 0.0).then_inc(zeroed, 1)
                pool.wait_ge(zeroed, 7 + b)
                for hh in range(GH):
                    ge(pool, v_set, GH * b + hh)
                    nc.gpsimd.memset(V[b][hh * WIN:(hh + 1) * WIN, :, :, GH * HD + hh:GH * HD + hh + 1],
                                     1.0).then_inc(v_set, 1)
                pool.wait_ge(v_set, GH * (b + 1))

            set_v(0)
            low_parts(0, 0)
            ln1_rstd(3, 2 * TILES, 4 * TILES)
            nc.gpsimd.memset(QS[1][:, 0].rearrange("p g h t -> p (g h t)").bitcast(U32), 0).then_inc(zeroed_pool, 1)
            low_parts(0, 1)
            ln1_rstd(4, 4 * TILES, NT)
            set_v(1)
            low_parts(1, 0)
            pool.wait_ge(rstd1_done, 3)
            ln1_norm(3, 1)
            nc.gpsimd.affine_select(out=shift[:], in_=ones[:], compare_op=ALU.is_equal, fill=0.0, base=1,
                                    pattern=[[-1, P]], channel_multiplier=1).then_inc(consts, 1)
            nc.gpsimd.affine_select(out=pick[:], in_=ones[:, 0:2 * HC], compare_op=ALU.is_equal, fill=0.0,
                                    base=-(LORA_AT + 1), pattern=[[-2, 2 * HC]],
                                    channel_multiplier=1).then_inc(consts, 1)
            pool.wait_ge(w_in, 16 * N_W)
            pool.wait_ge(x_rest, 16)
            add_bo(0, 2 * TILES)
            add_bo(2 * TILES, 4 * TILES)
            add_bo(4 * TILES, NT)
            low_parts(1, 1)
            pool.wait_ge(rstd1_done, 4)
            with pool.Fori(2, SUPER) as turn:
                for b in range(2):
                    ln1_norm(2 * turn + b, b)
                    low_parts(turn, b)

            def ln2_rstd(f):
                i0, i1 = f * FT, (f + 1) * FT
                pool.wait_ge(var2_done, f + 1)
                nc.gpsimd.tensor_tensor(rstd2[:, i0:i1], var2[:, i0:i1], half[:, i0:i1], ALU.pow).then_inc(rstd2_done, 1)

            def ln2_norm(f):
                pool.wait_ge(rstd2_done, f + 1)
                ge(pool, x2T_ps, f - 1)
                if f == 2:
                    pool.wait_ge(update_ps, 1)
                rows, x2 = slice(FT * f, FT * (f + 1)), xn2[f % 2]
                mean, rstd = (col.to_broadcast([P, FT, D]) for col in (mv2[:, rows, 0:1], rstd2[:, rows].unsqueeze(2)))
                nc.gpsimd.tensor_tensor(x2[:], x1[:, rows], mean, ALU.subtract).then_inc(x2_centred, 1)
                pool.wait_ge(x2_centred, f)
                nc.gpsimd.tensor_tensor(x2[:], x2[:], rstd, ALU.mult).then_inc(xn2_done, 1)

            def add_b2(f):
                i0, i1 = f * FT, (f + 1) * FT
                nc.gpsimd.tensor_tensor(x_bo[:, i0:i1], x1[:, i0:i1],
                                        b2_row[:].unsqueeze(1).to_broadcast([P, FT, D]),
                                        ALU.add).then_inc(x1b_done, 1)

            for f in range(NF):
                ln2_rstd(f)
                if f > 0:
                    ln2_norm(f)
                add_b2(f)

        @block.tensor
        def _(pe):
            def turn_weights():
                pe.wait_ge(w_in, 16 * N_W)
                pe.wait_ge(slots_set, 4)
                for c in range(HC):
                    nc.tensor.transpose(bank_o[0][:, c * P:(c + 1) * P], w1[:, c], ident[:])
                for c in range(HC):
                    mm = nc.tensor.transpose(bank_o[1][:, c * P:(c + 1) * P], w2[:, c * P:(c + 1) * P], ident[:])
                mm.then_inc(wT_ps, 1)

            def turn_x(c, b):
                pe.wait_ge(xn_done, c + 1)
                ge(pe, xT_done, c)
                for t in range(TILES):
                    mm = nc.tensor.transpose(bank_t[:, t * P:(t + 1) * P], xn[b][:, t], ident[:])
                mm.then_inc(xT_ps, 1)

            def project(c, b):
                pe.wait_ge(xT_done, c + 1)
                ge(pe, rest_done, c)
                nc.tensor.matmul(bank_qk[:, 0:CHUNK], wq[:], xT[b][:], start=True, stop=True)
                nc.tensor.matmul(bank_qk[:, CHUNK:], wk[:], xT[b][:], start=True, stop=True).then_inc(qk_ps, 1)

            def project_v(c, b):
                ge(pe, v_done, c)
                for t in range(TILES):
                    mm = nc.tensor.matmul(bank_v[:, t * D:(t + 1) * D], xT[b][:, t * P:(t + 1) * P], wv[:],
                                          start=True, stop=True)
                mm.then_inc(v_ps, 1)

            def mask_slots():
                pe.wait_ge(consts, 8)
                one_hot_cols = ident_bf[0:2 * WIN, 0:2 * WIN].rearrange("p (e q) -> p q e", e=2).unsqueeze(2)
                band_cols = band[:].unsqueeze(1)
                for s in range(2):
                    pick_rows = select[:, s].rearrange("p g r -> p (g r)")
                    nc.tensor.matmul(bank_o[0][:, s * CHUNK:(s + 1) * CHUNK].rearrange("p (q n e) -> p q n e", q=WIN, e=2),
                                     pick_rows, one_hot_cols.to_broadcast([2 * WIN, WIN, BLOCKS // 2, 2]),
                                     start=True, stop=True)
                    mm = nc.tensor.matmul(bank_o[1][:, s * CHUNK:(s + 1) * CHUNK].rearrange(
                        "p (n e q) -> p n e q", q=WIN, e=2), pick_rows,
                        band_cols.to_broadcast([2 * WIN, BLOCKS // 2, 2, WIN]), start=True, stop=True)
                mm.then_inc(slots_ps, 1)

            def scores(turn, s):
                k, b, u = SU * turn + s, s // UNITS, s % UNITS
                if u == 0:
                    pe.wait_ge(stacked[b], STACKS * turn + STACKS)
                ge(pe, probs_done, k - 1)
                for i in range(UB):
                    j = UB * u + i
                    for g in range(NG):
                        dst = bank_s[s % 2][:, (i * NG + g) * 2 * WIN:(i * NG + g + 1) * 2 * WIN]
                        for o in range(2):
                            mm = nc.tensor.matmul(dst, QS[b][:, o, g].rearrange("p h t -> p (h t)")[:, j::BLOCKS],
                                                  KS[b][:, o, g, j * WIN:(j + 2) * WIN],
                                                  start=(i == 0 and g == 0 and o == 0), stop=False,
                                                  skip_group_check=True)
                mm.then_inc(s_ps, 1)

            def centre(turn, s):
                k = SU * turn + s
                pe.wait_ge(max_parts, k + 1)
                for part, last in ((high_half(negmax[s % 2]), False), (negmax_low[s % 2][:], True)):
                    mm = nc.tensor.matmul(bank_s[s % 2][:].rearrange("p (a k) -> p a k", k=2 * WIN), ident_bf[:],
                                          part.unsqueeze(2).to_broadcast([P, UB * NG, 2 * WIN]),
                                          start=False, stop=last, skip_group_check=True)
                mm.then_inc(centred_ps, 1)

            def values(turn, s):
                k, b, u = SU * turn + s, s // UNITS, s % UNITS
                if u == 0:
                    c = 2 * turn + b
                    pe.wait_ge(v_done, c + 1)
                if isinstance(turn, int) and k == 0:
                    pe.wait_ge(wT_sb, 2)
                if s % 2 == 0:
                    ge(pe, att_done, (SU // 2) * turn + s // 2 - 1)
                pe.wait_ge(probsT_done, k + 1)
                o = bank_o[(s // 2) % 2]
                for i in range(UB):
                    j = UB * u + i
                    q = j % (P // WIN)
                    for g in range(NG):
                        for w in range(2):
                            mm = nc.tensor.matmul(o[q * WIN:(q + 1) * WIN, g * VC:(g + 1) * VC],
                                                  probsT[s % 2][:, i, g, w, :], V[b][:, j + w, g, :],
                                                  start=(w == 0), stop=(w == 1))
                mm.then_inc(pv_ps, 1)

            def turn_x2(f):
                pe.wait_ge(xn2_done, f + 1)
                ge(pe, x2T_done, f)
                for t in range(FT):
                    mm = nc.tensor.transpose(bank_t[:, t * P:(t + 1) * P], xn2[f % 2][:, t], ident[:])
                mm.then_inc(x2T_ps, 1)


            def up(f, c):
                pe.wait_ge(x2T_done, f + 1)
                if f == 0:
                    pe.wait_ge(*((weff_done, 2) if c < 2 else (probs_done, NU - 3 + c)))
                elif f == 1 and c < 2:
                    pe.wait_ge(att_done, NT - 1 + c)
                else:
                    pe.wait_ge(hidden_done, HC * (f - 1) + c + 1)
                nc.tensor.matmul(bank_h(f, c)[:], w1T[:, c * P:(c + 1) * P], x2T[f % 2][:],
                                 start=True, stop=True).then_inc(h_ps, 1)

            def even_tokens():
                nc.tensor.matmul(bank_qk[:, 0:D], shift[:], xn2[0][:, 0], start=True, stop=True).then_inc(even_ps, 1)

            def weight_update():
                pe.wait_ge(pairs_done, 2 * HC)
                pe.wait_ge(v_done, NCH)
                nc.tensor.matmul(bank_v[:], xn2[0][:, 0], pair1[:].rearrange("p t d -> p (t d)"),
                                 start=True, stop=True)
                nc.tensor.matmul(bank_qk[:], xn2[0][:, 0], pair2[:].rearrange("p c t i -> p (c t i)"),
                                 start=True, stop=True).then_inc(update_ps, 1)

            def turn_att(tile, odd):
                pe.wait_ge(att_done, tile + 1)
                ge(pe, x1_done, tile)
                nc.tensor.transpose(bank_w[:, 0:P], att[odd][:], ident[:]).then_inc(attT_ps, 1)

            def out_proj(tile):
                pe.wait_ge(attT_done, tile + 1)
                nc.tensor.matmul(bank_w[:, P:2 * P], attT[:], wo[:], start=True, stop=True).then_inc(wo_ps, 1)

            def step(turn, s, last):
                b, u = s // UNITS, s % UNITS
                first = isinstance(turn, int) and turn == 0
                p1 = projects(turn, b)
                tiles = SU // 2
                if not (first and s < 1) and s < SU + 1:
                    centre(turn if s >= 1 else turn - 1, (s - 1) % SU)
                if not (first and s < 3) and s < SU + 3:
                    values(turn if s >= 3 else turn - 1, (s - 3) % SU)
                if s % 2 == 1 and not (first and s < 7):
                    out_proj(tiles * turn + (s - 7) // 2)
                if s % 2 == 0 and not (first and s < 6) and s < SU + 5:
                    turn_att(tiles * turn + (s - 6) // 2, (s - 6) // 2 % 2)
                if s < SU:
                    c = 2 * turn + b
                    if p1 and u == 0:
                        turn_x(c + 2, b)
                if s < SU and p1 and u == 1:
                    project(c + 2, b)
                if s + 1 < SU:
                    scores(turn, s + 1)
                elif s + 1 == SU and not last:
                    scores(turn + 1, 0)
                if s < SU:
                    if not (last and b == 1) and u == 2:
                        project_v(c + 1, 1 - b)
                if last and s == 2:
                    turn_x2(0)
                    even_tokens()
                if last and s == 5:
                    weight_update()
                if last and s in (7, 8, 9, 10):
                    up(0, s - 7)
                if last and s == 7:
                    turn_x2(1)
                if last and s in (11, 12):
                    up(1, s - 11)

            mask_slots()
            turn_x(0, 0)
            pe.wait_ge(w_first, 16 * N_FIRST)
            nc.tensor.transpose(bank_v[:, 0:3 + HC], bias_rows[:], ident[0:3 + HC, 0:3 + HC]).then_inc(bias_ps, 1)
            project(0, 0)
            turn_x(1, 1)
            project(1, 1)
            pe.wait_ge(bias_done, 1)
            project_v(0, 0)
            turn_x(2, 0)
            project(2, 0)
            turn_weights()

            def body(turn):
                for s in range(SU):
                    step(turn, s, is_last(turn))

            scores(0, 0)
            turns(pe, body)
            for s in range(SU, SU + 6):
                step(SUPER - 1, s, True)

            def down(f):
                pe.wait_ge(hidden_done, HC * (f + 1))
                ge(pe, y_done, f - 1)
                for chunk, t0, t1, bank_y in PIECES:
                    if chunk != f:
                        continue
                    if bank_y is bank_t:
                        pe.wait_ge(x2T_done, NF)
                    for t in range(t0, t1):
                        for c in range(HC):
                            mm = nc.tensor.matmul(bank_y[:, t * D:(t + 1) * D],
                                                  hidden[f % 2][:, c, t * P:(t + 1) * P], w2T[:, c],
                                                  start=(c == 0), stop=(c == HC - 1))
                    mm.then_inc(y_ps, 1)

            for f in range(1, NF + 1):
                if f < NF:
                    for c in range(2 if f == 1 else 0, HC):
                        up(f, c)
                if f + 1 < NF:
                    turn_x2(f + 1)
                down(f - 1)

        @block.scalar
        def _(act):
            def ident_act(dst, src, **kw):
                return nc.scalar.activation(dst, src, ACT.Identity, **kw)

            def copy_xT(c, b):
                act.wait_ge(xT_ps, c + 1)
                ge(act, v_ps, c - 1)
                ident_act(xT[b][:], bank_t[:, 0:CHUNK]).then_inc(xT_done, 1)

            def high(turn, b):
                c = 2 * turn + b
                act.wait_ge(qk_ps, c + 1)
                if not (isinstance(turn, int) and turn == 0):
                    act.wait_ge(q_in[b], 16 * turn)
                    act.wait_ge(k_in[b], 16 * turn)
                ge(act, repeat_done, c)
                ident_act(q_parts[b][:, 2].rearrange("p (q n) -> p q n", q=WIN), by_query(bank_qk), bias=bqc)
                ident_act(k_parts[b][:, 1, WIN:], bank_qk[:, CHUNK:], bias=bkc).then_inc(high_done, 1)

            def middle(c, b):
                act.wait_ge(rest_done, c + 1)
                ident_act(q_parts[b][:, 0:2], rest[:, 0:1].to_broadcast([P, 2, CHUNK])).then_inc(mid_q_done, 1)
                ident_act(k_parts[b][:, 0:3:2, WIN:], rest[:, 1:2].to_broadcast([P, 2, CHUNK])).then_inc(mid_done, 1)

            def spread_v(turn, b, half_):
                c = 2 * turn + b
                if half_ == 0:
                    act.wait_ge(v_ps, c + 1)
                    ge(act, pv_ps, UNITS * (c - 1))
                    if isinstance(turn, int) and turn == 0:
                        act.wait_ge(v_set, GH * (b + 1))
                    if not (isinstance(turn, int) and turn == 0 and b == 0):
                        act.wait_ge(v_done, c)
                        ident_act(V[b][:, 0], V[1 - b][:, BLOCKS])
                blocks = P // WIN
                for q in range(2 * half_, 2 * half_ + 2):
                    for hh in range(GH):
                        dst = V[b][hh * WIN:(hh + 1) * WIN, 1 + q::blocks, :, hh * HD:(hh + 1) * HD]
                        src = bank_v[q * WIN:(q + 1) * WIN, 0:TILES * D].rearrange(
                            "p (t g h d) -> p t g h d", t=TILES, g=NG, h=GH)[:, :, :, hh]
                        cp = ident_act(dst, src)
                if half_ == 1:
                    cp.then_inc(v_done, 1)

            def token_pairs(layer, pairs):
                act.wait_ge(even_ps, 1)
                for t in range(HC):
                    out, src = ((pairs[:, t], bank_qk[:, 0:D]) if layer == 0 else
                                (pairs[:, :, t], bank_qk[:, 0:D].rearrange("p (i c) -> p c i", c=HC)))
                    i = layer * HC + t
                    ident_act(out, src, scale=pick[:, i:i + 1]).then_inc(pairs_done, 1)

            def softmax_exp(turn, s):
                k = SU * turn + s
                act.wait_ge(centred_ps, k + 1)
                ge(act, probsT_done, k - 1)
                nc.scalar.activation(probs[s % 2][:], bank_s[s % 2][:], ACT.Exp,
                                     scale=float(HD) ** -0.5).then_inc(probs_done, 1)

            def copy_attT(tile):
                act.wait_ge(attT_ps, tile + 1)
                ge(act, wo_ps, tile)
                ident_act(attT[:], bank_w[:, 0:P], bias=bvc).then_inc(attT_done, 1)

            def set_slots(b):
                ident_act(q_parts[b][:, MASK:], bank_o[0][:].rearrange("p (s t) -> p s t", s=2)).then_inc(slots_set, 1)
                ident_act(k_parts[b][:, MASK:, WIN:],
                          bank_o[1][:].rearrange("p (s t) -> p s t", s=2)).then_inc(slots_set, 1)

            act.wait_ge(slots_ps, 1)
            set_slots(0)
            copy_xT(0, 0)
            act.wait_ge(bias_ps, 1)
            ident_act(bias_cols[:], bank_v[:, 0:3 + HC]).then_inc(bias_done, 1)
            act.wait_ge(bias_done, 1)
            high(0, 0)
            copy_xT(1, 1)
            middle(0, 0)
            high(0, 1)
            set_slots(1)
            middle(1, 1)
            copy_xT(2, 0)
            high(1, 0)
            spread_v(0, 0, 0)
            middle(2, 0)

            def step(turn, s, last):
                b, u = s // UNITS, s % UNITS
                first = isinstance(turn, int) and turn == 0
                p1 = projects(turn, b)
                if s < SU:
                    c = 2 * turn + b
                    if p1 and u == 1:
                        copy_xT(c + 2, b)
                    if not (first and s == 0):
                        softmax_exp(turn if s >= 1 else turn - 1, (s - 1) % SU)
                    if p1 and u == 1:
                        high(turn + 1, b)
                elif s == SU:
                    softmax_exp(turn, SU - 1)
                if s % 2 == 0 and not (first and s < 6):
                    copy_attT((SU // 2) * turn + (s - 6) // 2)
                if first and s == 1:
                    act.wait_ge(wT_ps, 1)
                    ident_act(w1T[:], bank_o[0][:]).then_inc(wT_sb, 1)
                    ident_act(w2T[:].rearrange("p c o -> p (c o)"), bank_o[1][:]).then_inc(wT_sb, 1)
                if first and s == 2:
                    spread_v(0, 0, 1)
                if s < SU:
                    if p1 and u == 2:
                        middle(c + 2, b)
                    if not (last and b == 1) and u == 3:
                        spread_v(turn if b == 0 else turn + 1, 1 - b, 0)
                    if not (first and b == 0) and u == 0:
                        spread_v(turn, b, 1)
                    if last and s == 3:
                        token_pairs(0, pair1)
                    if last and s == 4:
                        token_pairs(1, pair2)

            def body(turn):
                for s in range(SU):
                    step(turn, s, is_last(turn))

            turns(act, body)
            def gelu(f, c):
                act.wait_ge(h_ps, HC * f + c + 1)
                nc.scalar.activation(hidden[f % 2][:, c], bank_h(f, c)[:], ACT.Gelu,
                                     bias=b1c[:, c:c + 1]).then_inc(hidden_done, 1)

            for s in range(SU, SU + 5):
                step(SUPER - 1, s, True)
                if s < SU + HC:
                    gelu(0, s - SU)
            for f in range(1, NF):
                ge(act, y_ps, f - 1)
                for c in range(HC):
                    gelu(f, c)

        @block.vector
        def _(dve):
            def set_one_hot():
                dve.wait_ge(consts, 2)
                for s in range(2):
                    cols = one_hot[:].rearrange("p (q s n e) -> p s q n e", s=2, n=BLOCKS // 2, e=2)[:, s]
                    rows = ident_bf[:].rearrange("p (e q c) -> p c q e", e=2, c=SLOTS // 2)[:, 2 + s]
                    nc.vector.tensor_copy(cols, rows.unsqueeze(2).to_broadcast(
                        [P, WIN // 2, BLOCKS // 2, 2])).then_inc(one_hot_set, 1)

            def set_q(b):
                nc.vector.tensor_copy(QS[b][:, 1].rearrange("p g h t -> p (g h) t"),
                                      one_hot[:].unsqueeze(1).to_broadcast([P, NG * GH, CHUNK])).then_inc(q_set, 1)

            def ln1_var(t0, t1):
                for t in range(t0, t1):
                    nc.vector.bn_stats(stats1[:, t], x_sb[:, t]).then_inc(dve_ln, 1)
                dve.wait_ge(dve_ln, t0 + t1)
                for t in range(t0, t1):
                    nc.vector.bn_aggr(mv1[:, t], stats1[:, t]).then_inc(dve_ln, 1)
                dve.wait_ge(dve_ln, 2 * t1)
                nc.vector.tensor_scalar(var1[:, t0:t1], mv1[:, t0:t1, 1], EPS, None, ALU.add).then_inc(var1_done, 1)

            def ln1_norm(c, b):
                ge(dve, xT_ps, c - 1)
                for t in range(TILES):
                    i = TILES * c + t
                    n = nc.vector.tensor_scalar(xn[b][:, t], x_sb[:, i], mv1[:, i, 0:1],
                                                rstd1[:, bass.ds(i, 1)], ALU.subtract, ALU.mult)
                n.then_inc(xn_done, 1)

            def split_rest(c, b):
                dve.wait_ge(high_done, c + 1)
                ge(dve, low_done, c)
                nc.vector.scalar_tensor_tensor(rest[:, 0].rearrange("p (q n) -> p q n", q=WIN), by_query(bank_qk), bqc,
                                               q_parts[b][:, 2].rearrange("p (q n) -> p q n", q=WIN),
                                               ALU.add, ALU.subtract)
                nc.vector.scalar_tensor_tensor(rest[:, 1], bank_qk[:, CHUNK:], bkc, k_parts[b][:, 1, WIN:],
                                               ALU.add, ALU.subtract).then_inc(rest_done, 1)

            def repeat_high(c, b):
                nc.vector.tensor_copy(q_parts[b][:, 3:5], q_parts[b][:, 2:3].to_broadcast([P, 2, CHUNK]))
                rep = nc.vector.tensor_copy(k_parts[b][:, 3:6:2, WIN:],
                                            k_parts[b][:, 1:2, WIN:].to_broadcast([P, 2, CHUNK]))
                if not (isinstance(c, int) and c == 0):
                    rep = nc.vector.tensor_copy(k_parts[b][:, :, 0:WIN], k_parts[1 - b][:, :, CHUNK:KW])
                rep.then_inc(repeat_done, 1)

            def row_max(turn, s):
                k = SU * turn + s
                dve.wait_ge(s_ps, k + 1)
                ge(dve, centred_ps, k - 1)
                nc.vector.tensor_reduce(negmax[s % 2][:], bank_s[s % 2][:].rearrange("p (a k) -> p a k", k=2 * WIN),
                                        AX.X, ALU.max, negate=True).then_inc(max_done, 1)

            def split_max(turn, s):
                dve.wait_ge(max_done, SU * turn + s + 1)
                nc.vector.tensor_tensor(negmax_low[s % 2][:], negmax[s % 2][:], high_half(negmax[s % 2]),
                                        ALU.subtract).then_inc(max_parts, 1)

            def turn_probs(turn, s):
                k = SU * turn + s
                dve.wait_ge(probs_done, k + 1)
                ge(dve, pv_ps, k - 1)
                nc.vector.transpose(probsT[s % 2][:].rearrange("p i g w q -> p (i g w q)"),
                                    probs[s % 2][:]).then_inc(probsT_done, 1)

            def heads_out(odd):
                return bank_o[odd][:, 0:NG * VC].rearrange("p (g c) -> p g c", g=NG)

            def denominators(tile, odd):
                dve.wait_ge(pv_ps, 2 * tile + 2)
                ge(dve, att_done, tile)
                nc.vector.reciprocal(rden[:], heads_out(odd)[:, :, GH * HD:]).then_inc(rden_done, 1)

            def normalise(tile, odd):
                dve.wait_ge(rden_done, tile + 1)
                ge(dve, attT_ps, tile - 1)
                nc.vector.tensor_tensor(att[odd][:].rearrange("p (g h d) -> p g h d", g=NG, h=GH),
                                        heads_out(odd)[:, :, 0:GH * HD].rearrange("p g (h d) -> p g h d", h=GH),
                                        rden[:].unsqueeze(3).to_broadcast([P, NG, GH, HD]),
                                        ALU.mult).then_inc(att_done, 1)

            def residual(tile):
                dve.wait_ge(wo_ps, tile + 1)
                dve.wait_ge(x_bo_done, 1 if isinstance(tile, int) and tile == 0 else 3)
                nc.vector.tensor_tensor(x1[:, tile], bank_w[:, P:2 * P], x_bo[:, tile], ALU.add).then_inc(x1_done, 1)

            def ln2_var(f):
                i0, i1 = f * FT, (f + 1) * FT
                dve.wait_ge(st2_done, i1)
                for i in range(i0, i1):
                    nc.vector.bn_aggr(mv2[:, i], stats2[:, i]).then_inc(mv2_done, 1)
                dve.wait_ge(mv2_done, i1)
                nc.vector.tensor_scalar(var2[:, i0:i1], mv2[:, i0:i1, 1], EPS, None, ALU.add).then_inc(var2_done, 1)

            def ln2_norm(f):
                dve.wait_ge(rstd2_done, f + 1)
                for t in range(FT):
                    i = FT * f + t
                    n = nc.vector.tensor_scalar(xn2[f % 2][:, t], x1[:, i], mv2[:, i, 0:1], rstd2[:, i:i + 1],
                                                ALU.subtract, ALU.mult)
                n.then_inc(xn2_done, 1)

            def copy_x2T(f):
                dve.wait_ge(x2T_ps, f + 1)
                ge(dve, h_ps, HC * (f - 1))
                nc.vector.tensor_copy(x2T[f % 2][:], bank_t[:]).then_inc(x2T_done, 1)

            def update_weights():
                dve.wait_ge(update_ps, 1)
                nc.vector.scalar_tensor_tensor(w1T[:], bank_v[:], scale_c[:], w1T[:], ALU.mult,
                                               ALU.add).then_inc(weff_done, 1)
                w2T_flat = w2T[:].rearrange("p c o -> p (c o)")
                nc.vector.scalar_tensor_tensor(w2T_flat, bank_qk[:], scale_c[:], w2T_flat, ALU.mult,
                                               ALU.add).then_inc(weff_done, 1)

            nc.vector.memset(QS[0][:, 0].rearrange("p g h t -> p (g h t)").bitcast(U32), 0).then_inc(q_set, 1)
            dve.wait_ge(x_first, 16)
            ln1_var(0, TILES)
            set_one_hot()
            dve.wait_ge(rstd1_done, 1)
            ln1_norm(0, 0)
            dve.wait_ge(x_second, 16)
            ln1_var(TILES, 2 * TILES)
            dve.wait_ge(one_hot_set, 2)
            set_q(0)
            dve.wait_ge(rstd1_done, 2)
            ln1_norm(1, 1)
            dve.wait_ge(bias_done, 1)
            split_rest(0, 0)
            repeat_high(0, 0)
            dve.wait_ge(x_rest, 16)
            ln1_var(2 * TILES, 4 * TILES)
            set_q(1)
            dve.wait_ge(slots_set, 4)
            split_rest(1, 1)
            repeat_high(1, 1)
            dve.wait_ge(rstd1_done, 3)
            ln1_norm(2, 0)
            ln1_var(4 * TILES, NT)
            split_rest(2, 0)
            repeat_high(2, 0)

            def step(turn, s, last):
                b, u = s // UNITS, s % UNITS
                first = isinstance(turn, int) and turn == 0
                p1 = projects(turn, b)
                tiles = SU // 2
                tile = tiles * turn + s // 2 - 4
                rows = s % 2 == 0 and not first
                out_tile = tiles * turn + (s - 5) // 2
                outs = s % 2 == 1 and not (first and s < 5) and s < SU + 4
                if rows:
                    dve.wait_ge(x1_done, tile + 1)
                if s < SU:
                    row_max(turn, s)
                if rows:
                    nc.vector.bn_stats(stats2[:, tile] if isinstance(tile, int) else stats2[:, bass.ds(tile, 1)],
                                       x1[:, tile]).then_inc(st2_done, 1)
                if outs:
                    denominators(out_tile, (s - 5) // 2 % 2)
                if s < SU:
                    split_max(turn, s)
                if s < SU and p1 and u == 2:
                    split_rest(2 * turn + b + 2, b)
                if not (first and s < 2) and s < SU + 2:
                    turn_probs(turn if s >= 2 else turn - 1, (s - 2) % SU)
                if s % 2 == 1 and not (first and s < 7):
                    residual(tiles * turn + (s - 7) // 2)
                if outs:
                    normalise(out_tile, (s - 5) // 2 % 2)
                if last and s in (0, 3):
                    ln2_var(s // 3)
                if last and s == 1:
                    ln2_norm(0)
                if last and s == 2:
                    copy_x2T(0)
                if last and s == 6:
                    update_weights()
                if last and s == 9:
                    copy_x2T(1)
                    ln2_var(2)
                if s < SU and p1 and u == 2:
                    repeat_high(2 * turn + b + 2, b)

            def body(turn):
                for s in range(SU):
                    step(turn, s, is_last(turn))

            turns(dve, body)
            for s in range(SU, SU + 7):
                step(SUPER - 1, s, True)

            ln2_var(3)
            copy_x2T(2)
            for n, (f, t0, t1, bank_y) in enumerate(PIECES):
                dve.wait_ge(x1b_done, f + 1)
                dve.wait_ge(y_ps, n + 1)
                ge(dve, stored[f % 2], 16 * (f // 2))
                nc.vector.tensor_tensor(y[f % 2][:, t0:t1].rearrange("p t d -> p (t d)"),
                                        bank_y[:, t0 * D:t1 * D],
                                        x_bo[:, f * FT + t0:f * FT + t1].rearrange("p t d -> p (t d)"),
                                        ALU.add).then_inc(y_done, 1)
                if f == 0:
                    copy_x2T(3)


_INS = ["L0_attn_x", "L0_attn_Wq", "L0_attn_bq", "L0_attn_Wk", "L0_attn_bk", "L0_attn_Wv", "L0_attn_bv",
        "L0_attn_Wo", "L0_attn_bo", "L0_ffn_W1", "L0_ffn_b1", "L0_ffn_W2", "L0_ffn_b2", "L0_ffn_scale"]


def kernel(**inputs):
    import numpy as _np
    import concourse.bacc as _bacc
    from concourse import mybir as _mybir
    from concourse.bass_utils import run_bass_kernel_spmd as _run

    nc = _bacc.Bacc("TRN2", target_bir_lowering=False, num_devices=1)
    arrays, args = {}, []
    for name in _INS:
        a = _np.ascontiguousarray(inputs[name])
        if a.ndim == 0:
            a = a.reshape(1)
        arrays[f"in_{name}_dram"] = a
        args.append(nc.dram_tensor(f"in_{name}_dram", a.shape, _mybir.dt.from_np(a.dtype), kind="ExternalInput").ap())
    shape = inputs["L0_attn_x"].shape
    args.append(nc.dram_tensor("out_0_dram", shape, F32, kind="ExternalOutput").ap())
    block_kernel(nc, *args)
    r = _run(nc, [arrays], core_ids=[0])
    return r.results[0]["out_0_dram"]
```
